# Optimizing a Trainium2 kernel written in Bass

```python
import numpy as np
import jax
import jax.numpy as jnp

def _softmax(x, axis=-1):
    return jax.nn.softmax(x, axis=axis)

def _gelu(x):
    return jax.nn.gelu(x, approximate=True)

def _silu(x):
    return jax.nn.silu(x)

def _sigmoid(x):
    return jax.nn.sigmoid(x)

def _layernorm(x, axis=-1, eps=1e-05):
    m = jnp.mean(x, axis=axis, keepdims=True)
    v = jnp.var(x, axis=axis, keepdims=True)
    return (x - m) / jnp.sqrt(v + eps)

def _scatter_add(tgt, idx, src, axis=0):
    return tgt.at[idx].add(src)

def _segment_sum(src, seg, n):
    return jax.ops.segment_sum(src, seg, n)
kernel_name = 'mk_recurrent_d1_jaxref_r8_f07194'

def setup_inputs(seed: int=0):
    np.random.seed(seed)
    _w = jnp.asarray

    def _L0_attn_setup():
        import jax, jax.numpy as jnp
        import numpy as np
        key = jax.random.key(seed)
        ks = jax.random.split(key, 5)
        B, S, D = (1, 512, 256)
        H, Dh = (16, 128)
        scale = 1.0 / np.sqrt(D).astype(np.float32)
        return {'x': jax.random.normal(ks[0], (B, S, D), dtype=jnp.float32), 'W_K': jax.random.normal(ks[1], (H, Dh, D), dtype=jnp.float32) * scale, 'W_Q': jax.random.normal(ks[2], (H, Dh, D), dtype=jnp.float32) * scale, 'W_V': jax.random.normal(ks[3], (H, Dh, D), dtype=jnp.float32) * scale, 'W_O': jax.random.normal(ks[4], (D, H * Dh), dtype=jnp.float32) * scale}
    _L0_attn_in = _L0_attn_setup()

    def _L0_ffn_setup():
        import jax, jax.numpy as jnp
        import numpy as np
        B_, S, D = (4, 512, 256)
        OUT = 256
        E, R = (8, 16)
        ALPHA = 32.0
        SCALING = ALPHA / R
        key = jax.random.key(seed)
        ks = jax.random.split(key, 6)
        x = jax.random.normal(ks[0], (B_, S, D), dtype=jnp.float32)
        W_base = jax.random.normal(ks[1], (OUT, D), dtype=jnp.float32) * D ** (-0.5)
        b_base = jax.random.normal(ks[2], (OUT,), dtype=jnp.float32) * 0.01
        router_W = jax.random.normal(ks[3], (E, D), dtype=jnp.float32) * D ** (-0.5)
        A = jax.random.normal(ks[4], (E, R, D), dtype=jnp.float32) * D ** (-0.5)
        Bw = jax.random.normal(ks[5], (E, OUT, R), dtype=jnp.float32) * 0.02
        return {'x': x, 'W_base': W_base, 'b_base': b_base, 'router_W': router_W, 'A': A, 'Bw': Bw}
    _L0_ffn_in = _L0_ffn_setup()
    _d = {'L0_attn_x': _L0_attn_in['x'], 'L0_attn_W_K': _L0_attn_in['W_K'], 'L0_attn_W_Q': _L0_attn_in['W_Q'], 'L0_attn_W_V': _L0_attn_in['W_V'], 'L0_attn_W_O': _L0_attn_in['W_O'], 'L0_ffn_W_base': _L0_ffn_in['W_base'], 'L0_ffn_b_base': _L0_ffn_in['b_base'], 'L0_ffn_router_W': _L0_ffn_in['router_W'], 'L0_ffn_A': _L0_ffn_in['A'], 'L0_ffn_Bw': _L0_ffn_in['Bw']}
    _x0 = _d['L0_attn_x']
    _d['L0_attn_x'] = jax.random.normal(jax.random.fold_in(jax.random.key(seed), 1), (1, 2048, 256), dtype=_x0.dtype)
    del _x0
    return _d

def reference(L0_attn_x, L0_attn_W_K, L0_attn_W_Q, L0_attn_W_V, L0_attn_W_O, L0_ffn_W_base, L0_ffn_b_base, L0_ffn_router_W, L0_ffn_A, L0_ffn_Bw):

    def _L0_attn_ref(x, W_K, W_Q, W_V, W_O):
        import jax, jax.numpy as jnp
        import numpy as np
        b, pos, d_model = x.shape
        d_head = W_K.shape[1]
        k = jnp.einsum('ihd,bpd->biph', W_K, x)
        q = jnp.einsum('ihd,bpd->biph', W_Q, x)
        v = jnp.einsum('ihd,bpd->biph', W_V, x)
        scores = jnp.einsum('biph,biqh->biqp', k, q)
        mask = jnp.tril(jnp.ones((pos, pos), dtype=x.dtype))
        masked = scores * mask - jnp.float32(10000000000.0) * (1.0 - mask)
        attn = jax.nn.softmax(masked / jnp.sqrt(jnp.float32(d_head)), axis=-1)
        z = jnp.einsum('biqp,biph->biqh', attn, v)
        z_flat = jnp.transpose(z, (0, 2, 1, 3)).reshape(b, pos, -1)
        out = jnp.einsum('df,bqf->bqd', W_O, z_flat)
        return out

    def _L0_ffn_ref(x, W_base, b_base, router_W, A, Bw):
        import jax, jax.numpy as jnp
        import numpy as np
        B_, S, D = (4, 512, 256)
        OUT = 256
        E, R = (8, 16)
        ALPHA = 32.0
        SCALING = ALPHA / R
        base_out = jnp.einsum('bsd,od->bso', x, W_base) + b_base
        logits = jnp.einsum('bsd,ed->bse', jax.lax.stop_gradient(x), router_W)
        routing_probs = jax.nn.softmax(logits, axis=-1)
        expert_idx = jnp.argmax(routing_probs, axis=-1)
        onehot = jax.nn.one_hot(expert_idx, E, dtype=x.dtype)
        h = jnp.einsum('bsd,erd->bser', x, A)
        h = h * onehot[..., None]
        delta = jnp.einsum('bser,eor->bso', h, Bw)
        return base_out + delta * SCALING
    x = L0_attn_x
    xn = _layernorm(x, axis=-1)
    s = _L0_attn_ref(xn, L0_attn_W_K, L0_attn_W_Q, L0_attn_W_V, L0_attn_W_O)
    g = _silu(_L0_ffn_ref(xn, L0_ffn_W_base, L0_ffn_b_base, L0_ffn_router_W, L0_ffn_A, L0_ffn_Bw))
    x = x + s * g
    return x

_drawn_inputs = setup_inputs


def setup_inputs(seed=0):
    import zlib

    import numpy as np

    out = dict(_drawn_inputs(seed))
    spreads = {}
    factors = {'L0_ffn_b_base': 25.325}
    for name, (base, spread) in spreads.items():
        noise = np.random.default_rng([zlib.crc32(name.encode()), seed]).standard_normal(out[name].shape)
        drawn = base * np.exp(spread * noise) if base else spread * noise
        out[name] = jnp.asarray(drawn.astype(out[name].dtype))
    for name, factor in factors.items():
        out[name] = (out[name] * factor).astype(out[name].dtype)
    return out
```

```python
from collections import namedtuple
from contextlib import ExitStack

import concourse.bass as bass
from concourse import mybir

ALU = mybir.AluOpType
ACT = mybir.ActivationFunctionType
AX = mybir.AxisListType.X
F32 = mybir.dt.float32
F32R = mybir.dt.float32r
BF16 = mybir.dt.bfloat16

P = 128
TB = 4
BW = TB * P
LAG = 3
PROBS = LAG + 1
SCORE_BANKS = 3
AUX_BANKS = 3
MASKED = -1.0e10
SCALING = 2.0
EPS = 1e-5

Score = namedtuple("Score", "n head g kt")
Value = namedtuple("Value", "n head g kt")
RowMax = namedtuple("RowMax", "aux head g q c last")
Project = namedtuple("Project", "aux ev which head b")
ProjectV = namedtuple("ProjectV", "aux ev b half")
SplitZ = namedtuple("SplitZ", "gi")
Sums = namedtuple("Sums", "aux gi")
Out = namedtuple("Out", "aux gi half")
Normed = namedtuple("Normed", "aux ev c b")


def number(kinds):
    plan, aux, ev = [], 0, 0
    for kind, args in kinds:
        if kind in (Normed, Project, ProjectV):
            plan.append(kind(aux, ev, *args))
            ev += 1
        elif kind in (RowMax, Sums, Out):
            plan.append(kind(aux, *args))
        else:
            plan.append(kind(*args))
            continue
        aux += 1
    return plan, aux, ev


def row_maxes(head, g):
    jobs = [(q, c) for c in range(g + 1) for q in range(TB)]
    return [(RowMax, (head, g, q, c, k == len(jobs) - 1)) for k, (q, c) in enumerate(jobs)]


def plan_start(NB):
    kinds = [(Normed, (c, b)) for b in range(NB) for c in range(2)]
    kinds += [(Project, (w, 0, b)) for b in range(2) for w in "kq"]
    return number(kinds + row_maxes(0, 0))


def plan_pair(NB, last):
    steps = [(h, g, kt) for h in range(2) for g in range(NB) for kt in range(TB * (g + 1))]
    kinds, n, closing = [], 0, []
    for h in range(2):
        for g in range(NB):
            fill = []
            if h == 0:
                fill += [(ProjectV, (b, half)) for b in {0: (0, 1), 1: (2,), 2: (3,)}.get(g, ()) for half in range(2)]
            ahead = (h, g + 2) if g + 2 < NB else (h + 1, g + 2 - NB)
            nxt = (h, g + 1) if g + 1 < NB else (h + 1, 0)
            maxes = row_maxes(*nxt) if not (last and nxt[0] == 2) else []
            proj = [(Project, (w, *ahead)) for w in "kq"] if not (last and ahead[0] == 2) else []
            tail = []
            if h == 1 and g == NB - 1:
                tail, proj = proj, []
            half = len(maxes) // 2
            fill += maxes[:half] + proj + maxes[half:]
            count = TB * (g + 1)
            spread = count - 3 if h == 1 and g == NB - 1 else count
            done = 0
            for s in range(count):
                kinds.append((Score, (n, *steps[n])))
                if n >= LAG:
                    m = n - LAG
                    kinds.append((Value, (m, *steps[m])))
                    if closing:
                        kinds.append(closing.pop(0))
                    if m + 1 < len(steps) and steps[m + 1][:2] != steps[m][:2]:
                        gi = steps[m][0] * NB + steps[m][1]
                        kinds.append((SplitZ, (gi,)))
                        closing = [(Sums, (gi,)), (Out, (gi, 0)), (Out, (gi, 1))]
                upto = min(len(fill), -(-len(fill) * (s + 1) // spread))
                kinds += fill[done:upto]
                done = max(done, upto)
                n += 1
    for m in range(len(steps) - LAG, len(steps)):
        kinds.append((Value, (m, *steps[m])))
    gi = 2 * NB - 1
    kinds.append((SplitZ, (gi,)))
    kinds += tail[:1] + [(Sums, (gi,))] + tail[1:] + [(Out, (gi, 0)), (Out, (gi, 1))]
    return number(kinds)


def attention_layer(nc, x, wqk, wv, wo, ffn_w, lora_b, bias, out):
    S, D = x.shape[1], x.shape[2]
    DC = D // P
    NT, NB = S // P, S // BW
    H = wqk.shape[1]
    PAIRS = H // 2
    E = 8
    R = lora_b.shape[0] // E
    FW = D + E + E * R
    SCALE = float(P) ** -0.5
    assert DC == 2 and NT == TB * NB and H % 2 == 0 and E * R == P

    start_plan, START_AUX, START_EV = plan_start(NB)
    pair_plan, PAIR_AUX, PAIR_EV = plan_pair(NB, False)
    last_plan, LAST_AUX, LAST_EV = plan_pair(NB, True)
    TILES = 2 * TB * NB * (NB + 1) // 2
    GROUPS = 2 * NB

    with ExitStack() as ctx:
        def sb(name, shape, dt=F32):
            return ctx.enter_context(nc.sbuf_tensor(name, shape, dt))

        def sem(name):
            return ctx.enter_context(nc.semaphore(name))

        xT_hi, xT_lo = (sb(f"xT_{s}", [P, DC, S], F32R) for s in ("hi", "lo"))
        kT_hi, kT_lo = (sb(f"kT_{s}", [P, 6, BW], F32R) for s in ("hi", "lo"))
        qT_hi, qT_lo = (sb(f"qT_{s}", [P, NB, BW], F32R) for s in ("hi", "lo"))
        v_hi, v_lo = (sb(f"v_{s}", [P, NT, 2 * P], F32R) for s in ("hi", "lo"))
        probs = sb("probs", [P, PROBS, BW])
        p_hi, p_lo = (sb(f"p_{s}", [P, PROBS, BW], F32R) for s in ("hi", "lo"))
        z_hi, z_lo = (sb(f"z_{s}", [P, BW], F32R) for s in ("hi", "lo"))
        colsum = sb("colsum", [P, 2, BW])
        cs_hi, cs_lo = (sb(f"cs_{s}", [P, BW], F32R) for s in ("hi", "lo"))
        shift = sb("shift", [P, 2, TB, P], F32R)
        partmax = sb("partmax", [P, 2, TB, NB])
        rowmax = sb("rowmax", [P, 2, TB])
        rinv = sb("rinv", [P, 2, TB])
        acc = sb("acc", [P, NT, D])
        wraw = sb("wraw", [P, 3, BW])
        wqk_hi, wqk_lo = (sb(f"wqk_{s}", [P, 2, 2, DC, P], F32R) for s in ("hi", "lo"))
        wv_hi, wv_lo = (sb(f"wv_{s}", [P, DC, 2 * P], F32R) for s in ("hi", "lo"))
        wo_hi, wo_lo = (sb(f"wo_{s}", [P, 2, D], F32R) for s in ("hi", "lo"))
        ident = sb("ident", [P, P])
        neg_ident = sb("neg_ident", [P, P])
        ident_bf = sb("ident_bf", [P, P], BF16)
        mask_bf = sb("mask_bf", [P, P], BF16)
        mask_rows = sb("mask_rows", [P, BW])
        zeros = sb("zeros", [P, P])
        wait_slot = sb("wait_slot", [P, AUX_BANKS])
        ones = sb("ones", [P, P])
        ones_r = sb("ones_r", [P, P], F32R)
        stats = sb("stats", [P, NT, 6])
        moments = sb("moments", [P, NT, 2])
        rstd = sb("rstd", [P, 6, NT])
        rank = sb("rank", [P, TB, E])
        route = sb("route", [P, 6, TB, E])
        routed = sb("routed", [P, TB, E * R])
        rT_hi, rT_lo = (sb(f"rT_{s}", [P, TB, P], F32R) for s in ("hi", "lo"))
        gate = sb("gate", [P, 2, TB, D])
        masked_row = gate[:, :, :, :].rearrange("p a t d -> p (a t d)")[:, 0:AUX_BANKS * BW]\
            .rearrange("p (k n) -> p k n", k=AUX_BANKS)

        ps = ctx.enter_context(nc.psum_tensor("ps", [P, 8, BW], F32))
        st = [ps[:, k, :] for k in range(SCORE_BANKS)]
        zb = [ps[:, SCORE_BANKS + k, :] for k in range(2)]
        aux = [ps[:, SCORE_BANKS + 2 + k, :] for k in range(AUX_BANKS)]

        x_in = [sem(f"x_in{b}") for b in range(NB)]
        wqk_in, wv_in, wo_in = sem("wqk_in"), sem("wv_in"), sem("wo_in")
        weight_hi = sem("weight_hi")
        wqk_ready, wv_ready, wo_ready = sem("wqk_ready"), sem("wv_ready"), sem("wo_ready")
        consts = sem("consts")
        made = sem("made")
        moments_done = sem("moments_done")
        sqrt_done = sem("sqrt_done")
        normed = sem("normed")
        acc_zero = sem("acc_zero")
        aux_full = sem("aux_full")
        aux_hi = sem("aux_hi")
        aux_free = sem("aux_free")
        max_ready = sem("max_ready")
        shift_ready = sem("shift_ready")
        scores_ready = sem("scores_ready")
        probs_ready = sem("probs_ready")
        hi_ready = sem("hi_ready")
        lo_ready = sem("lo_ready")
        sum_done = sem("sum_done")
        z_full = sem("z_full")
        z_hi_ready, z_lo_ready = sem("z_hi_ready"), sem("z_lo_ready")
        cs_hi_ready, cs_lo_ready = sem("cs_hi_ready"), sem("cs_lo_ready")
        rinv_ready = sem("rinv_ready")
        ffn_in = sem("ffn_in")
        ffn_w_ready = sem("ffn_w_ready")
        base_full = sem("base_full")
        routing = sem("routing")
        routed_ready = sem("routed_ready")
        routedT = sem("routedT")
        routedT_hi, routedT_lo = sem("routedT_hi"), sem("routedT_lo")
        lora_done = sem("lora_done")
        biased = sem("biased")
        gated = sem("gated")
        x_again = [sem(f"x_again{k}") for k in range(2)]
        attended = sem("attended")
        result = sem("result")
        stored = sem("stored")

        def k_slot(head, b):
            return NB + b if head % 2 and b < 2 else b

        def columns(t):
            return P * (t.kt % TB) if t.kt // TB == t.g else 0

        def tiles_until(gi):
            return sum(TB * (k % NB + 1) for k in range(gi + 1))

        def mm3(dst, w_hi, w_lo, m_hi, m_lo, first=True, last=True):
            nc.tensor.matmul(dst, w_hi, m_hi, start=first, stop=False)
            nc.tensor.matmul(dst, w_hi, m_lo, start=False, stop=False)
            return nc.tensor.matmul(dst, w_lo, m_hi, start=False, stop=last)

        def f32(ap):
            return ap.bitcast(F32)

        def evacuated(job):
            src = aux[job.aux % AUX_BANKS]
            if isinstance(job, Normed):
                cols = slice(job.b * BW, (job.b + 1) * BW)
                return src, xT_hi[:, job.c, cols], xT_lo[:, job.c, cols]
            if isinstance(job, ProjectV):
                t = TB * job.b + 2 * job.half
                return (src.rearrange("p (t n) -> p t n", t=2), v_hi[:, t:t + 2, :], v_lo[:, t:t + 2, :])
            hi, lo = (qT_hi, qT_lo) if job.which == "q" else (kT_hi, kT_lo)
            slot = job.b if job.which == "q" else k_slot(job.head, job.b)
            return src, hi[:, slot, :], lo[:, slot, :]

        block = ctx.enter_context(nc.Block())

        @block.sync
        def _(sp):
            xt = x[0].rearrange("(b t p) d -> b p t d", p=P, t=TB)
            for b in range(NB):
                sp.dma_start(acc[:, TB * b:TB * (b + 1), :], xt[b]).then_inc(x_in[b], 16)
                if b == 0:
                    sp.dma_start(wraw[:, 0, :], wqk[:, 0, :]).then_inc(wqk_in, 16)
                    sp.dma_start(wraw[:, 1, :], wv[:, 0, :]).then_inc(wv_in, 16)
                    sp.dma_start(wraw[:, 2, :], wo[:, 0, :]).then_inc(wo_in, 16)

            def loads(i, last):
                sp.wait_ge(wqk_ready, 2 * i + 1)
                sp.dma_start(wraw[:, 0, :], wqk[:, 2 * i + 1, :] if last else
                             wqk[:, bass.ds(2 * i + 1, 1), :].rearrange("p a n -> p (a n)")).then_inc(wqk_in, 16)
                if last:
                    return
                for raw, src, ready, arrived in ((1, wv, wv_ready, wv_in), (2, wo, wo_ready, wo_in)):
                    sp.wait_ge(ready, i + 1)
                    sp.dma_start(wraw[:, raw, :], src[:, bass.ds(i + 1, 1), :].rearrange("p a n -> p (a n)"))\
                      .then_inc(arrived, 16)
                sp.wait_ge(wqk_ready, 2 * i + 2)
                sp.dma_start(wraw[:, 0, :], wqk[:, bass.ds(2 * i + 2, 1), :].rearrange("p a n -> p (a n)"))\
                  .then_inc(wqk_in, 16)

            with sp.Fori(0, PAIRS - 1) as i:
                loads(i, False)
            loads(PAIRS - 1, True)
            sp.wait_ge(wqk_ready, H)
            sp.wait_ge(wv_ready, PAIRS)
            sp.wait_ge(wo_ready, PAIRS)
            for c in range(DC):
                sp.dma_start(wraw[:, c, 0:FW], ffn_w[:, c, :]).then_inc(ffn_in, 16)
            sp.dma_start(wraw[:, 2, 0:D], lora_b).then_inc(ffn_in, 16)
            sp.dma_start(wraw[:, 2, D:2 * D], bias.partition_broadcast(P)).then_inc(ffn_in, 16)
            out_t = out[0].rearrange("(b t p) d -> b p t d", p=P, t=TB)
            sp.wait_ge(lo_ready, PAIRS * TILES)
            sp.wait_ge(sum_done, PAIRS * TILES)
            for b in range(NB):
                k = b % 2
                if b >= 2:
                    sp.wait_ge(result, b - 1)
                sp.dma_start(probs[:, 2 * k:2 * k + 2, :].rearrange("p a (t d) -> p (a t) d", d=D), xt[b])\
                  .then_inc(x_again[k], 16)
                if b:
                    sp.wait_ge(result, b)
                    sp.dma_start(out_t[b - 1], acc[:, TB * (b - 1):TB * b, :]).then_inc(stored, 16)
            sp.wait_ge(result, NB)
            sp.dma_start(out_t[NB - 1], acc[:, TB * (NB - 1):, :]).then_inc(stored, 16)
            sp.wait_ge(stored, 16 * NB)

        @block.gpsimd
        def _(pool):
            splits = [0]

            def split_weights(raw, hi, lo, arrived, count, nth, ready):
                pool.wait_ge(arrived, count)
                nc.gpsimd.tensor_tensor(hi, raw, zeros[:, 0:1].broadcast_to([P, raw.shape[-1]]), ALU.add)\
                  .then_inc(weight_hi, 1)
                pool.wait_ge(weight_hi, nth)
                nc.gpsimd.tensor_tensor(lo, raw, f32(hi), ALU.subtract).then_inc(ready, 1)

            def flat(t):
                return t.rearrange("p a b -> p (a b)") if len(t.shape) == 3 else t.rearrange("p a b c -> p (a b c)")

            nc.gpsimd.memset(ident[:, :], 0.0).then_inc(made, 1)
            nc.gpsimd.memset(neg_ident[:, :], 0.0).then_inc(made, 1)
            nc.gpsimd.memset(ident_bf[:, :], 0.0).then_inc(made, 1)
            nc.gpsimd.memset(mask_bf[:, :], 0.0).then_inc(made, 1)
            nc.gpsimd.memset(mask_rows[:, :], 0.0).then_inc(made, 1)
            nc.gpsimd.memset(zeros[:, :], 0.0)
            nc.gpsimd.memset(ones[:, :], 1.0).then_inc(made, 1)
            for e in range(E):
                nc.gpsimd.memset(rank[:, :, e:e + 1], float(E - e))
            pool.wait_ge(made, 6)
            diagonal = dict(compare_op=ALU.not_equal, base=0, pattern=[[-1, P]], channel_multiplier=1)
            nc.gpsimd.affine_select(out=ident[:, :], in_=ident[:, :], fill=1.0, **diagonal)
            nc.gpsimd.affine_select(out=neg_ident[:, :], in_=neg_ident[:, :], fill=-1.0, **diagonal)
            nc.gpsimd.affine_select(out=ident_bf[:, :], in_=ident_bf[:, :], fill=1.0, **diagonal)
            nc.gpsimd.affine_select(out=mask_bf[:, :], in_=mask_bf[:, :], compare_op=ALU.is_ge, fill=MASKED,
                                    base=0, pattern=[[1, P]], channel_multiplier=-1)
            nc.gpsimd.affine_select(out=mask_rows[:, BW - P:], in_=mask_rows[:, BW - P:], compare_op=ALU.is_ge,
                                    fill=MASKED, base=0, pattern=[[-1, P]], channel_multiplier=1)
            nc.gpsimd.tensor_copy(ones_r[:, :], ones[:, :]).then_inc(consts, 1)
            split_weights(wraw[:, 0, :], flat(wqk_hi[:, 0]), flat(wqk_lo[:, 0]), wqk_in, 16, 1, wqk_ready)
            split_weights(wraw[:, 1, :], flat(wv_hi[:, :, :]), flat(wv_lo[:, :, :]), wv_in, 16, 2, wv_ready)

            def make_shift(job, block_no):
                pool.wait_ge(max_ready, block_no)
                k = job.g % 2
                nc.gpsimd.tensor_tensor(
                    shift[:, k, :, :], neg_ident[:, None, :].broadcast_to([P, TB, P]),
                    rowmax[:, k, :][:, :, None].broadcast_to([P, TB, P]), ALU.mult).then_inc(shift_ready, 1)

            for job in start_plan:
                if isinstance(job, RowMax) and job.last:
                    pool.wait_ge(aux_full, len([j for j in start_plan if isinstance(j, Normed)]))
                    nc.gpsimd.memset(acc[:, :, :], 0.0).then_inc(acc_zero, 1)
                    make_shift(job, 1)

            def pair(i, plan, last):
                groups = 1
                for job in plan:
                    if isinstance(job, RowMax) and job.last:
                        groups += 1
                        make_shift(job, i * GROUPS + groups)
                    if not isinstance(job, Score):
                        continue
                    n, c0 = job.n, columns(job)
                    gi = job.head * NB + job.g
                    total, tile = colsum[:, gi % 2, :], probs[:, n % PROBS, :]
                    pool.wait_ge(probs_ready, i * TILES + n + 1)
                    if job.kt == 0:
                        if job.g == 0:
                            nc.gpsimd.tensor_tensor(total[:, 0:P], tile[:, 0:P], zeros[:, :], ALU.add)
                    elif job.kt == 1:
                        before = probs[:, (n - 1) % PROBS, :]
                        nc.gpsimd.tensor_tensor(total[:, c0:], before[:, c0:], tile[:, c0:], ALU.add)\
                          .then_inc(sum_done, 2)
                    else:
                        pool.wait_ge(sum_done, i * TILES + n)
                        nc.gpsimd.tensor_tensor(total[:, c0:], total[:, c0:], tile[:, c0:], ALU.add)\
                          .then_inc(sum_done, 1)
                    hi_no = 4 * i + 2
                    if n == 1:
                        split_weights(wraw[:, 2, :], flat(wo_hi[:, :, :]), flat(wo_lo[:, :, :]),
                                      wo_in, 16 * (i + 1), hi_no + 1, wo_ready)
                    if n == 6:
                        split_weights(wraw[:, 0, :], flat(wqk_hi[:, 1]), flat(wqk_lo[:, 1]),
                                      wqk_in, 16 * (2 * i + 2), hi_no + 2, wqk_ready)
                    if n == TILES // 2 + 6 and not last:
                        split_weights(wraw[:, 0, :], flat(wqk_hi[:, 0]), flat(wqk_lo[:, 0]),
                                      wqk_in, 16 * (2 * i + 3), hi_no + 3, wqk_ready)
                    if n == TILES // 2 + 14 and not last:
                        split_weights(wraw[:, 1, :], flat(wv_hi[:, :, :]), flat(wv_lo[:, :, :]),
                                      wv_in, 16 * (i + 2), hi_no + 4, wv_ready)

            with pool.Fori(0, PAIRS - 1) as i:
                pair(i, pair_plan, False)
            pair(PAIRS - 1, last_plan, True)

            hi_no = 4 * (PAIRS - 1) + 4
            for c in range(DC):
                split_weights(wraw[:, c, 0:FW], flat(wqk_hi[:, c])[:, 0:FW], flat(wqk_lo[:, c])[:, 0:FW],
                              ffn_in, 64, hi_no + c + 1, ffn_w_ready)
            split_weights(wraw[:, 2, 0:D], wv_hi[:, 0, :], wv_lo[:, 0, :], ffn_in, 64, hi_no + DC + 1, ffn_w_ready)

        @block.scalar
        def _(act):
            act.wait_ge(moments_done, 1)
            nc.scalar.activation(rstd[:, 1, :], rstd[:, 0, :], ACT.Sqrt).then_inc(sqrt_done, 1)

            def walk(plan, i, aux0, ev0):
                groups = 0
                for job in plan:
                    if isinstance(job, (Normed, Project, ProjectV)):
                        src, hi, _ = evacuated(job)
                        act.wait_ge(aux_full, aux0 + job.aux + 1)
                        nc.scalar.activation(hi, src, ACT.Copy).then_inc(aux_hi, 1)
                    elif isinstance(job, Score):
                        n, c0 = job.n, columns(job)
                        k = n % PROBS
                        act.wait_ge(scores_ready, i * TILES + n + 1)
                        if n >= PROBS:
                            act.wait_ge(sum_done, i * TILES + n - PROBS + 1)
                        src = st[n % SCORE_BANKS][:, c0:]
                        nc.scalar.activation(probs[:, k, c0:], src, ACT.Exp, scale=SCALE).then_inc(probs_ready, 1)
                        nc.scalar.activation(p_hi[:, k, c0:], src, ACT.Exp, scale=SCALE).then_inc(hi_ready, 1)
                    elif isinstance(job, SplitZ):
                        groups += 1
                        act.wait_ge(z_full, i * GROUPS + groups)
                        nc.scalar.activation(z_hi[:, :], zb[job.gi % 2], ACT.Copy).then_inc(z_hi_ready, 1)
                        act.wait_ge(sum_done, i * TILES + tiles_until(job.gi))
                        nc.scalar.activation(cs_hi[:, :], colsum[:, job.gi % 2, :], ACT.Copy)\
                          .then_inc(cs_hi_ready, 1)

            walk(start_plan, 0, 0, 0)
            with act.Fori(0, PAIRS - 1) as i:
                walk(pair_plan, i, START_AUX + i * PAIR_AUX, 0)
            walk(last_plan, PAIRS - 1, START_AUX + (PAIRS - 1) * PAIR_AUX, 0)

            for b in range(NB):
                act.wait_ge(routedT, b + 1)
                nc.scalar.activation(rT_hi[:, :, :].rearrange("p t n -> p (t n)"), aux[b % 2], ACT.Copy)\
                  .then_inc(routedT_hi, 1)
                act.wait_ge(biased, b + 1)
                g = gate[:, b % 2, :, :]
                nc.scalar.activation(g, g, ACT.Silu).then_inc(gated, 1)

        @block.vector
        def _(dve):
            for b in range(NB):
                dve.wait_ge(x_in[b], 16)
                for t in range(TB * b, TB * (b + 1)):
                    op = nc.vector.bn_stats(stats[:, t, :], acc[:, t, :])
            op.then_inc(normed, 1)
            dve.wait_ge(normed, 1)
            for t in range(NT):
                op = nc.vector.bn_aggr(moments[:, t, :], stats[:, t, :])
            op.then_inc(normed, 1)
            dve.wait_ge(normed, 2)
            nc.vector.tensor_scalar(rstd[:, 0, :], moments[:, :, 1], EPS, None, ALU.add).then_inc(moments_done, 1)
            dve.wait_ge(sqrt_done, 1)
            r, v = rstd[:, 2, :], rstd[:, 0, :]
            nc.vector.reciprocal(r, rstd[:, 1, :]).then_inc(normed, 1)
            dve.wait_ge(normed, 3)
            nc.vector.tensor_tensor(rstd[:, 3, :], r, r, ALU.mult).then_inc(normed, 1)
            dve.wait_ge(normed, 4)
            nc.vector.scalar_tensor_tensor(rstd[:, 4, :], rstd[:, 3, :], -0.5, v, ALU.mult, ALU.mult)\
              .then_inc(normed, 1)
            dve.wait_ge(normed, 5)
            nc.vector.scalar_tensor_tensor(rstd[:, 5, :], rstd[:, 4, :], 1.5, r, ALU.add, ALU.mult)\
              .then_inc(normed, 1)
            dve.wait_ge(normed, 6)
            for t in range(NT):
                nc.vector.tensor_scalar(acc[:, t, :], acc[:, t, :], moments[:, t, 0:1], rstd[:, 5, t:t + 1],
                                        ALU.subtract, ALU.mult).then_inc(normed, 1)
            dve.wait_ge(consts, 1)

            def lo_part(i, n, c0):
                k = n % PROBS
                dve.wait_ge(hi_ready, i * TILES + n + 1)
                nc.vector.tensor_tensor(p_lo[:, k, c0:], probs[:, k, c0:], f32(p_hi[:, k, c0:]), ALU.subtract)\
                  .then_inc(lo_ready, 1)

            def walk(plan, i, aux0, ev0, maxima, first_groups):
                waiting, groups = [], 0
                for job in plan:
                    if isinstance(job, (Normed, Project, ProjectV)):
                        src, hi, lo = evacuated(job)
                        dve.wait_ge(aux_hi, ev0 + job.ev + 1)
                        nc.vector.tensor_tensor(lo, src, f32(hi), ALU.subtract).then_inc(aux_free, 1)
                    elif isinstance(job, RowMax):
                        src = aux[job.aux % AUX_BANKS]
                        dst = partmax[:, job.g % 2, job.q, job.c:job.c + 1]
                        dve.wait_ge(aux_full, aux0 + job.aux + 1)
                        if job.c < job.g:
                            nc.vector.reduce_max(dst, src, axis=AX).then_inc(aux_free, 1)
                        else:
                            w = P * (job.q + 1)
                            k = job.aux % AUX_BANKS
                            nc.vector.memset(wait_slot[:, k:k + 1], 0.0)
                            nc.vector.tensor_tensor_reduce(
                                out=masked_row[:, k, 0:w], in0=src[:, 0:w], in1=mask_rows[:, BW - w:], scale=1.0,
                                scalar=-3.0e38, op0=ALU.add, op1=ALU.max, accum_out=dst).then_inc(aux_free, 1)
                        if job.last:
                            groups += 1
                            dve.wait_ge(aux_free, aux0 + job.aux + 1)
                            nc.vector.reduce_max(rowmax[:, job.g % 2, :], partmax[:, job.g % 2, :, 0:job.g + 1],
                                                 axis=AX).then_inc(max_ready, 1)
                    elif isinstance(job, Score):
                        if waiting:
                            lo_part(i, *waiting.pop(0))
                        waiting.append((job.n, columns(job)))
                    elif isinstance(job, Value):
                        while waiting and waiting[0][0] <= job.n:
                            lo_part(i, *waiting.pop(0))
                    elif isinstance(job, SplitZ):
                        done = i * GROUPS + job.gi + 1
                        dve.wait_ge(z_hi_ready, done)
                        nc.vector.tensor_tensor(z_lo[:, :], zb[job.gi % 2], f32(z_hi[:, :]), ALU.subtract)\
                          .then_inc(z_lo_ready, 1)
                        dve.wait_ge(cs_hi_ready, done)
                        nc.vector.tensor_tensor(cs_lo[:, :], colsum[:, job.gi % 2, :], f32(cs_hi[:, :]),
                                                ALU.subtract).then_inc(cs_lo_ready, 1)
                    elif isinstance(job, Sums):
                        dve.wait_ge(aux_full, aux0 + job.aux + 1)
                        src = aux[job.aux % AUX_BANKS][:, 0:2 * TB].rearrange("p (t k) -> p t k", k=2)
                        nc.vector.reciprocal(rinv[:, job.gi % 2, :], src[:, :, 0]).then_inc(aux_free, 1)
                    elif isinstance(job, Out):
                        dve.wait_ge(aux_full, aux0 + job.aux + 1)
                        if job.half == 0:
                            sums_aux = max(j.aux for j in plan if isinstance(j, Sums) and j.gi == job.gi)
                            dve.wait_ge(aux_free, aux0 + sums_aux + 1)
                        for k in range(2):
                            q = 2 * job.half + k
                            dst = acc[:, TB * (job.gi % NB) + q, :]
                            op = nc.vector.scalar_tensor_tensor(
                                dst, aux[job.aux % AUX_BANKS][:, k * D:(k + 1) * D],
                                rinv[:, job.gi % 2, q:q + 1], dst, ALU.mult, ALU.add)
                        op.then_inc(aux_free, 1)

            walk(start_plan, 0, 0, 0, 0, 0)
            dve.wait_ge(acc_zero, 1)
            with dve.Fori(0, PAIRS - 1) as i:
                walk(pair_plan, i, START_AUX + i * PAIR_AUX, START_EV + i * PAIR_EV, 1, 0)
            walk(last_plan, PAIRS - 1, START_AUX + (PAIRS - 1) * PAIR_AUX, START_EV + (PAIRS - 1) * PAIR_EV, 1, 0)

            def bcast(ap, k):
                return ap[:, :, None].broadcast_to([P, TB, k])

            for b in range(NB):
                banks = ps[:, TB * (b % 1):TB * (b % 1) + TB, :]
                dve.wait_ge(base_full, b + 1)
                logits, step = banks[:, :, D:D + E], 6 * b

                def chain(op):
                    nonlocal step
                    step += 1
                    op.then_inc(routing, 1)
                    dve.wait_ge(routing, step)
                chain(nc.vector.reduce_max(route[:, 0, :, 0], logits, axis=AX))
                chain(nc.vector.tensor_tensor(route[:, 1], logits, bcast(route[:, 0, :, 0], E), ALU.is_equal))
                chain(nc.vector.tensor_tensor(route[:, 2], route[:, 1], rank[:, :, :], ALU.mult))
                chain(nc.vector.reduce_max(route[:, 3, :, 0], route[:, 2], axis=AX))
                chain(nc.vector.tensor_tensor(route[:, 4], route[:, 2], bcast(route[:, 3, :, 0], E), ALU.is_equal))
                chain(nc.vector.tensor_scalar(route[:, 5], route[:, 4], SCALING, None, ALU.mult))
                for t in range(TB):
                    op = nc.vector.tensor_tensor(
                        routed[:, t, :].rearrange("p (e r) -> p e r", e=E),
                        banks[:, t, D + E:FW].rearrange("p (e r) -> p e r", e=E),
                        route[:, 5, t, :][:, :, None].broadcast_to([P, E, R]), ALU.mult)
                op.then_inc(routed_ready, 1)
                dve.wait_ge(routedT_hi, b + 1)
                nc.vector.tensor_tensor(rT_lo[:, :, :].rearrange("p t n -> p (t n)"), aux[b % 2],
                                        f32(rT_hi[:, :, :].rearrange("p t n -> p (t n)")), ALU.subtract)\
                  .then_inc(routedT_lo, 1)
                dve.wait_ge(lora_done, b + 1)
                g, a = gate[:, b % 2, :, :], acc[:, TB * b:TB * (b + 1), :]
                nc.vector.tensor_tensor(g, banks[:, :, 0:D],
                                        wraw[:, 2, D:2 * D][:, None, :].broadcast_to([P, TB, D]), ALU.add)\
                  .then_inc(biased, 1)
                dve.wait_ge(gated, b + 1)
                nc.vector.tensor_tensor(a, a, g, ALU.mult).then_inc(attended, 1)
                dve.wait_ge(attended, b + 1)
                dve.wait_ge(x_again[b % 2], 16 * (b // 2 + 1))
                k = b % 2
                nc.vector.tensor_tensor(a, a, probs[:, 2 * k:2 * k + 2, :].rearrange("p a (t d) -> p (a t) d", d=D),
                                        ALU.add).then_inc(result, 1)

        @block.tensor
        def _(pe):
            pe.wait_ge(consts, 1)

            def walk(plan, i, aux0, start):
                made = {}
                for job in plan:
                    if hasattr(job, "aux"):
                        dst = aux[job.aux % AUX_BANKS]
                        if not (start and job.aux < AUX_BANKS):
                            pe.wait_ge(aux_free, aux0 + max(job.aux - AUX_BANKS + 1, 0))
                    if isinstance(job, Normed):
                        for t in range(TB):
                            tok = TB * job.b + t
                            pe.wait_ge(normed, 6 + tok + 1)
                            op = nc.tensor.transpose(dst[:, t * P:(t + 1) * P],
                                                     acc[:, tok, job.c * P:(job.c + 1) * P], ident[:, :])
                        op.then_inc(aux_full, 1)
                        made["x", 0, job.b] = job.aux
                    elif isinstance(job, Project):
                        if start:
                            pe.wait_ge(wqk_ready, 1)
                            pe.wait_ge(aux_free, aux0 + made["x", 0, job.b] + 1)
                        else:
                            pe.wait_ge(wqk_ready, 2 * i + job.head + 1)
                        w, par = "qk".index(job.which), job.head % 2
                        cols = slice(job.b * BW, (job.b + 1) * BW)
                        for c in range(DC):
                            op = mm3(dst, wqk_hi[:, par, w, c, :], wqk_lo[:, par, w, c, :],
                                     xT_hi[:, c, cols], xT_lo[:, c, cols], c == 0, c == DC - 1)
                        op.then_inc(aux_full, 1)
                        made["qk", job.head, job.b] = job.aux
                    elif isinstance(job, ProjectV):
                        pe.wait_ge(wv_ready, i + 1)
                        for t in range(2):
                            tok = TB * job.b + 2 * job.half + t
                            tile = slice(tok * P, (tok + 1) * P)
                            for c in range(DC):
                                op = mm3(dst[:, t * 2 * P:(t + 1) * 2 * P], xT_hi[:, c, tile], xT_lo[:, c, tile],
                                         wv_hi[:, c, :], wv_lo[:, c, :], c == 0, c == DC - 1)
                        op.then_inc(aux_full, 1)
                        made["v", 0, job.b] = job.aux
                    elif isinstance(job, RowMax):
                        if job.q == 0 and job.c == 0:
                            at = made.get(("qk", job.head, job.g))
                            pe.wait_ge(aux_free, aux0 + (at + 1 if at is not None else 0))
                        w = P * (job.q + 1) if job.c == job.g else BW
                        nc.tensor.matmul(dst[:, 0:w], qT_hi[:, job.g, job.q * P:(job.q + 1) * P],
                                         kT_hi[:, k_slot(job.head, job.c), 0:w], start=True, stop=True)\
                          .then_inc(aux_full, 1)
                    elif isinstance(job, Score):
                        n, c0 = job.n, columns(job)
                        if job.kt == 0:
                            pe.wait_ge(shift_ready, i * GROUPS + job.head * NB + job.g + 1)
                        if n >= SCORE_BANKS:
                            pe.wait_ge(hi_ready, i * TILES + n - SCORE_BANKS + 1)
                        dst = st[n % SCORE_BANKS][:, c0:]
                        slot, tile = k_slot(job.head, job.kt // TB), slice(P * (job.kt % TB), P * (job.kt % TB + 1))
                        mm3(dst, kT_hi[:, slot, tile], kT_lo[:, slot, tile], qT_hi[:, job.g, c0:],
                            qT_lo[:, job.g, c0:], True, False)
                        if job.kt // TB == job.g:
                            nc.tensor.matmul(dst[:, 0:P], ident_bf[:, :], mask_bf[:, :], start=False, stop=False)
                        nc.tensor.matmul(dst, ones_r[:, :],
                                         shift[:, job.g % 2, :, :].rearrange("p t n -> p (t n)")[:, c0:],
                                         start=False, stop=True).then_inc(scores_ready, 1)
                    elif isinstance(job, Value):
                        n, c0 = job.n, columns(job)
                        gi, k = job.head * NB + job.g, n % PROBS
                        at = made.get(("v", 0, job.kt // TB))
                        if job.head == 0 and job.kt == TB * job.g:
                            pe.wait_ge(aux_free, aux0 + at + 1)
                        pe.wait_ge(lo_ready, i * TILES + n + 1)
                        dst = zb[gi % 2][:, c0:]
                        cols = slice(P * job.head, P * (job.head + 1))
                        op = mm3(dst, v_hi[:, job.kt, cols], v_lo[:, job.kt, cols], p_hi[:, k, c0:],
                                 p_lo[:, k, c0:], job.kt == 0, job.kt == TB * (job.g + 1) - 1)
                        if job.kt == TB * (job.g + 1) - 1:
                            op.then_inc(z_full, 1)
                    elif isinstance(job, Sums):
                        pe.wait_ge(cs_lo_ready, i * GROUPS + job.gi + 1)
                        for q in range(TB):
                            tile = slice(q * P, (q + 1) * P)
                            nc.tensor.matmul(dst[:, 2 * q:2 * q + 2], cs_hi[:, tile], ones_r[:, 0:2],
                                             start=True, stop=False)
                            op = nc.tensor.matmul(dst[:, 2 * q:2 * q + 2], cs_lo[:, tile], ones_r[:, 0:2],
                                                  start=False, stop=True)
                        op.then_inc(aux_full, 1)
                    elif isinstance(job, Out):
                        pe.wait_ge(wo_ready, i + 1)
                        pe.wait_ge(z_lo_ready, i * GROUPS + job.gi + 1)
                        for k in range(2):
                            tile = slice((2 * job.half + k) * P, (2 * job.half + k + 1) * P)
                            op = mm3(dst[:, k * D:(k + 1) * D], z_hi[:, tile], z_lo[:, tile],
                                     wo_hi[:, job.gi // NB, :], wo_lo[:, job.gi // NB, :])
                        op.then_inc(aux_full, 1)

            walk(start_plan, 0, 0, True)
            with pe.Fori(0, PAIRS - 1) as i:
                walk(pair_plan, i, START_AUX + i * PAIR_AUX, False)
            walk(last_plan, PAIRS - 1, START_AUX + (PAIRS - 1) * PAIR_AUX, False)

            pe.wait_ge(ffn_w_ready, DC + 1)
            pe.wait_ge(aux_free, START_AUX + (PAIRS - 1) * PAIR_AUX + LAST_AUX)
            for b in range(NB):
                if b:
                    pe.wait_ge(biased, b)
                for t in range(TB):
                    tok = TB * b + t
                    tile = slice(tok * P, (tok + 1) * P)
                    for c in range(DC):
                        w_hi, w_lo = (w[:, c].rearrange("p a b c -> p (a b c)")[:, 0:FW] for w in (wqk_hi, wqk_lo))
                        op = mm3(ps[:, t, 0:FW], xT_hi[:, c, tile], xT_lo[:, c, tile], w_hi, w_lo,
                                 c == 0, c == DC - 1)
                op.then_inc(base_full, 1)
                pe.wait_ge(routed_ready, b + 1)
                for t in range(TB):
                    op = nc.tensor.transpose(aux[b % 2][:, t * P:(t + 1) * P], routed[:, t, :], ident[:, :])
                op.then_inc(routedT, 1)
                pe.wait_ge(routedT_lo, b + 1)
                for t in range(TB):
                    dst = ps[:, t, 0:D]
                    for k, (a, w) in enumerate(((rT_hi, wv_hi), (rT_hi, wv_lo), (rT_lo, wv_hi))):
                        op = nc.tensor.matmul(dst, a[:, t, :], w[:, 0, :], start=False, stop=k == 2,
                                              skip_group_check=True)
                op.then_inc(lora_done, 1)


def kernel(L0_attn_x, L0_attn_W_K, L0_attn_W_Q, L0_attn_W_V, L0_attn_W_O, L0_ffn_W_base, L0_ffn_b_base,
           L0_ffn_router_W, L0_ffn_A, L0_ffn_Bw):
    import numpy as np
    import concourse.bacc as bacc
    from concourse.bass_utils import run_bass_kernel_spmd

    f = np.ascontiguousarray
    x = f(np.asarray(L0_attn_x))
    H, Dh, D = L0_attn_W_Q.shape
    DC = D // 128

    def chunked(w):
        w = np.asarray(w)
        w = w.reshape(w.shape[:-1] + (DC, 128))
        return np.moveaxis(w, (-1, -2), (0, -2))

    wqk = f(np.stack([chunked(L0_attn_W_Q), chunked(L0_attn_W_K)], axis=2)).reshape(128, H, 2 * DC * Dh)
    wv = chunked(np.asarray(L0_attn_W_V).reshape(H // 2, 2 * Dh, D))
    wv = f(wv).reshape(128, H // 2, DC * 2 * Dh)
    wo = f(np.asarray(L0_attn_W_O).reshape(D, H, Dh).transpose(2, 1, 0)).reshape(Dh, H // 2, 2 * D)
    E, R, _ = L0_ffn_A.shape
    ffn_w = np.concatenate([np.asarray(L0_ffn_W_base), np.asarray(L0_ffn_router_W),
                            np.asarray(L0_ffn_A).reshape(E * R, D)], axis=0)
    ffn_w = f(chunked(ffn_w))
    lora_b = f(np.asarray(L0_ffn_Bw).transpose(0, 2, 1)).reshape(E * R, D)
    arrays = {"x": x, "wqk": wqk, "wv": wv, "wo": wo, "ffn_w": ffn_w, "lora_b": lora_b,
              "bias": f(np.asarray(L0_ffn_b_base))}

    nc = bacc.Bacc("TRN2", target_bir_lowering=False, num_devices=1)
    args = [nc.dram_tensor(f"{n}_dram", a.shape, mybir.dt.from_np(a.dtype), kind="ExternalInput").ap()
            for n, a in arrays.items()]
    out = nc.dram_tensor("out_dram", x.shape, mybir.dt.from_np(x.dtype), kind="ExternalOutput").ap()
    attention_layer(nc, *args, out)
    r = run_bass_kernel_spmd(nc, [{f"{n}_dram": a for n, a in arrays.items()}], core_ids=[0])
    return r.results[0]["out_dram"]
```

```python
from collections import namedtuple
from contextlib import ExitStack

import concourse.bass as bass
from concourse import mybir

ALU = mybir.AluOpType
ACT = mybir.ActivationFunctionType
AX = mybir.AxisListType.X
F32 = mybir.dt.float32
F32R = mybir.dt.float32r
BF16 = mybir.dt.bfloat16

P = 128
TB = 4
BW = TB * P
LAG = 3
PROBS = LAG + 1
SCORE_BANKS = 3
AUX_BANKS = 3
MASKED = -1.0e10
SCALING = 2.0
EPS = 1e-5

Score = namedtuple("Score", "n head g kt")
Value = namedtuple("Value", "n head g kt")
RowMax = namedtuple("RowMax", "aux head g q c last")
Project = namedtuple("Project", "aux ev which head b")
ProjectV = namedtuple("ProjectV", "aux ev b half")
SplitZ = namedtuple("SplitZ", "gi")
Sums = namedtuple("Sums", "aux gi")
Out = namedtuple("Out", "aux gi half")
Normed = namedtuple("Normed", "aux ev c b")
Base = namedtuple("Base", "b")


def number(kinds):
    plan, aux, ev = [], 0, 0
    for kind, args in kinds:
        if kind in (Normed, Project, ProjectV):
            plan.append(kind(aux, ev, *args))
            ev += 1
        elif kind in (RowMax, Sums, Out):
            plan.append(kind(aux, *args))
        else:
            plan.append(kind(*args))
            continue
        aux += 1
    return plan, aux, ev


def row_maxes(head, g, blocks=None):
    return [(RowMax, (head, g, q, c)) for c in (range(g + 1) if blocks is None else blocks) for q in range(TB)]


def mark_last(kinds):
    left = {}
    for kind, args in kinds:
        if kind is RowMax:
            left[args[:2]] = left.get(args[:2], 0) + 1
    whole = {args[:2] for kind, args in kinds if kind is RowMax and args[3] == args[1]}
    marked = []
    for kind, args in kinds:
        if kind is RowMax:
            left[args[:2]] -= 1
            args += (left[args[:2]] == 0 and args[:2] in whole,)
        marked.append((kind, args))
    return marked


def plan_start(NB):
    kinds = [(Normed, (c, b)) for b in range(NB) for c in range(2)]
    kinds += [(Project, (w, 0, b)) for b in range(2) for w in "kq"] + [(Project, ("q", 0, 2))]
    return number(mark_last(kinds + row_maxes(0, 0) + row_maxes(0, 1) + row_maxes(0, 2, (0, 1))))


def plan_pair(NB, last):
    steps = [(h, g, kt) for h in range(2) for g in range(NB) for kt in range(TB * (g + 1))]
    HEAD = len(steps) // 2
    begin = [steps.index((0, g, 0)) for g in range(NB)] + [HEAD]
    jobs = []

    def add(release, deadline, *kinds):
        for kind, args in kinds:
            head = {Project: args[1], RowMax: args[0]}.get(kind, 0)
            if not (last and head == 2):
                jobs.append((deadline, release, kind, args))

    for b in range(NB):
        for half in range(2):
            add(0, max(begin[b] + TB * b + LAG - 2, 1), (ProjectV, (b, half)))
    for h in range(2):
        at = h * HEAD
        add(at + 1, at + 5, (Project, ("k", h, 2)))
        add(at + 1, at + 7, (Project, ("q", h, 3)))
        add(at + 1, at + begin[2], (Project, ("k", h, 3)))
        add(at + 6, at + begin[2] - 4, *row_maxes(h, 2, (2,)))
        add(at + 8, at + begin[3] - 5, *row_maxes(h, 3, range(3)))
        add(at + begin[2] + 1, at + begin[3] - 4, *row_maxes(h, 3, (3,)))
        nxt = at + begin[2]
        add(nxt + 1, nxt + 6, (Project, ("q", h + 1, 0)), (Project, ("k", h + 1, 0)))
        add(nxt + 1, nxt + 9, (Project, ("q", h + 1, 1)))
        add(nxt + 1, nxt + 16, (Project, ("k", h + 1, 1)))
        add(at + begin[3] + 1, at + begin[3] + 6, (Project, ("q", h + 1, 2)))
        add(nxt + 7, at + HEAD - 6, *row_maxes(h + 1, 0))
        add(nxt + 10, at + HEAD - 4, *row_maxes(h + 1, 1, (0,)))
        add(nxt + 17, at + HEAD - 3, *row_maxes(h + 1, 1, (1,)))
        second = row_maxes(h + 1, 2, (0, 1))
        between = second[4:] if h == 1 and not last else []
        add(at + begin[3] + 7, at + HEAD - 1, *[job for job in second if job not in between])

    width = [BW - P * (kt % TB) if kt // TB == g else BW for _, g, kt in steps]
    slots = 2 * len(steps)
    pe = [(4.0 if k % 2 == 0 else 3.0) * width[max(k // 2 - LAG * (k % 2), 0)] for k in range(slots)]
    dve = [1.1 * width[k // 2] * (k % 2) for k in range(slots)]
    for n, step in enumerate(steps):
        if step[2] == 0 and n:
            for k, (a, b) in enumerate(((0, 1200), (2048, 100), (1536, 700), (1536, 700))):
                slot = min(2 * (n + LAG - 1 + k) + 1, slots - 1)
                pe[slot] += a
                dve[slot] += b
    cost = {Project: (3072, 640), ProjectV: (3072, 640), RowMax: (BW, 560)}

    def strain(k):
        total = 0.0
        for size in (1, 3, 6):
            for a in range(max(k - size + 1, 1 - size), min(k, slots - 1) + 1):
                window = slice(max(a, 0), min(a + size, slots))
                total += sum(dve[window]) ** 2 / sum(pe[window])
        return total

    def put(job, k, sign):
        a, b = cost[job[2]]
        pe[k] += sign * a
        dve[k] += sign * b

    def clipped(k):
        return min(max(k, 0), slots - 1)

    at = [clipped(job[0] + job[1]) for job in jobs]
    for job, k in zip(jobs, at):
        put(job, k, 1)
    for _ in range(4):
        for j, job in enumerate(jobs):
            put(job, at[j], -1)
            best = None
            for k in range(clipped(2 * job[1]), clipped(2 * job[0] + 1) + 1):
                before = strain(k)
                put(job, k, 1)
                rise = strain(k) - before
                put(job, k, -1)
                if best is None or rise < best[0]:
                    best = (rise, k)
            at[j] = best[1]
            put(job, at[j], 1)
    filled = [[] for _ in range(slots)]
    for job, k in sorted(zip(jobs, at), key=lambda a: a[0][0]):
        filled[k].append(job[2:])

    kinds, closing = [], []
    for n, step in enumerate(steps):
        kinds += [(Score, (n, *step))] + filled[2 * n]
        m = n - LAG
        if m >= 0:
            kinds.append((Value, (m, *steps[m])))
        if closing:
            kinds.append(closing.pop(0))
        if m >= 0 and steps[m + 1][:2] != steps[m][:2]:
            gi = steps[m][0] * NB + steps[m][1]
            kinds.append((SplitZ, (gi,)))
            closing = [(Sums, (gi,)), (Out, (gi, 0)), (Out, (gi, 1))]
        kinds += filled[2 * n + 1]
    assert not closing
    for k, m in enumerate(range(len(steps) - LAG, len(steps))):
        kinds += between[k:k + 1] + [(Value, (m, *steps[m]))]
    gi = 2 * NB - 1
    if last:
        between = [None] * LAG + [(Base, (0,))]
    kinds += [(SplitZ, (gi,))] + between[LAG:] + [(Sums, (gi,)), (Out, (gi, 0)), (Out, (gi, 1))]
    return number(mark_last(kinds))


def attention_layer(nc, x, wqk, wv, wo, ffn_w, lora_b, bias, out):
    S, D = x.shape[1], x.shape[2]
    DC = D // P
    NT, NB = S // P, S // BW
    H = wqk.shape[1]
    PAIRS = H // 2
    E = 8
    R = lora_b.shape[0] // E
    FW = D + E + E * R
    SCALE = float(P) ** -0.5
    assert DC == 2 and NT == TB * NB and H % 2 == 0 and E * R == P

    start_plan, START_AUX, START_EV = plan_start(NB)
    pair_plan, PAIR_AUX, PAIR_EV = plan_pair(NB, False)
    last_plan, LAST_AUX, LAST_EV = plan_pair(NB, True)
    TILES = 2 * TB * NB * (NB + 1) // 2
    GROUPS = 2 * NB

    with ExitStack() as ctx:
        def sb(name, shape, dt=F32):
            return ctx.enter_context(nc.sbuf_tensor(name, shape, dt))

        def sem(name):
            return ctx.enter_context(nc.semaphore(name))

        xT_hi, xT_lo = (sb(f"xT_{s}", [P, DC, S], F32R) for s in ("hi", "lo"))
        kT_hi, kT_lo = (sb(f"kT_{s}", [P, 6, BW], F32R) for s in ("hi", "lo"))
        qT_hi, qT_lo = (sb(f"qT_{s}", [P, NB, BW], F32R) for s in ("hi", "lo"))
        v_hi, v_lo = (sb(f"v_{s}", [P, NT, 2 * P], F32R) for s in ("hi", "lo"))
        probs = sb("probs", [P, PROBS, BW])
        p_hi, p_lo = (sb(f"p_{s}", [P, PROBS, BW], F32R) for s in ("hi", "lo"))
        z_hi, z_lo = (sb(f"z_{s}", [P, BW], F32R) for s in ("hi", "lo"))
        colsum = sb("colsum", [P, 2, BW])
        cs_hi, cs_lo = (sb(f"cs_{s}", [P, BW], F32R) for s in ("hi", "lo"))
        shift = sb("shift", [P, NB, TB, P], F32R)
        partmax = sb("partmax", [P, NB, TB, NB])
        rowmax = sb("rowmax", [P, NB, TB])
        rinv = sb("rinv", [P, 2, TB])
        acc = sb("acc", [P, NT, D])
        wraw = sb("wraw", [P, 3, BW])
        wqk_hi, wqk_lo = (sb(f"wqk_{s}", [P, 2, 2, DC, P], F32R) for s in ("hi", "lo"))
        wv_hi, wv_lo = (sb(f"wv_{s}", [P, DC, 2 * P], F32R) for s in ("hi", "lo"))
        wo_hi, wo_lo = (sb(f"wo_{s}", [P, 2, D], F32R) for s in ("hi", "lo"))
        ident = sb("ident", [P, P])
        neg_ident = sb("neg_ident", [P, P])
        ident_bf = sb("ident_bf", [P, P], BF16)
        mask_bf = sb("mask_bf", [P, P], BF16)
        mask_rows = sb("mask_rows", [P, BW])
        zeros = sb("zeros", [P, P])
        wait_slot = sb("wait_slot", [P, AUX_BANKS])
        ones = sb("ones", [P, P])
        ones_r = sb("ones_r", [P, P], F32R)
        stats = sb("stats", [P, NT, 6])
        moments = sb("moments", [P, NT, 2])
        rstd = sb("rstd", [P, 6, NT])
        rank = sb("rank", [P, TB, E])
        route = sb("route", [P, 6, TB, E])
        routed = sb("routed", [P, TB, E * R])
        rT_hi, rT_lo = (sb(f"rT_{s}", [P, TB, P], F32R) for s in ("hi", "lo"))
        gate = sb("gate", [P, 2, TB, D])
        masked_row = gate[:, :, :, :].rearrange("p a t d -> p (a t d)")[:, 0:AUX_BANKS * BW]\
            .rearrange("p (k n) -> p k n", k=AUX_BANKS)

        ps = ctx.enter_context(nc.psum_tensor("ps", [P, 8, BW], F32))
        st = [ps[:, k, :] for k in range(SCORE_BANKS)]
        zb = [ps[:, SCORE_BANKS + k, :] for k in range(2)]
        aux = [ps[:, SCORE_BANKS + 2 + k, :] for k in range(AUX_BANKS)]

        x_in = [sem(f"x_in{b}") for b in range(NB)]
        wqk_in, wv_in, wo_in = sem("wqk_in"), sem("wv_in"), sem("wo_in")
        weight_hi = sem("weight_hi")
        wqk_ready, wv_ready, wo_ready = sem("wqk_ready"), sem("wv_ready"), sem("wo_ready")
        consts = sem("consts")
        made = sem("made")
        moments_done = sem("moments_done")
        sqrt_done = sem("sqrt_done")
        normed = sem("normed")
        acc_zero = sem("acc_zero")
        aux_full = sem("aux_full")
        aux_hi = sem("aux_hi")
        aux_free = sem("aux_free")
        max_ready = sem("max_ready")
        shift_ready = sem("shift_ready")
        scores_ready = sem("scores_ready")
        probs_ready = sem("probs_ready")
        hi_ready = sem("hi_ready")
        lo_ready = sem("lo_ready")
        sum_done = sem("sum_done")
        z_full = sem("z_full")
        z_hi_ready, z_lo_ready = sem("z_hi_ready"), sem("z_lo_ready")
        cs_hi_ready, cs_lo_ready = sem("cs_hi_ready"), sem("cs_lo_ready")
        rinv_ready = sem("rinv_ready")
        ffn_in = sem("ffn_in")
        ffn_w_ready = sem("ffn_w_ready")
        base_full = sem("base_full")
        routing = sem("routing")
        routed_ready = sem("routed_ready")
        routedT = sem("routedT")
        routedT_hi, routedT_lo = sem("routedT_hi"), sem("routedT_lo")
        lora_done = sem("lora_done")
        gated = sem("gated")
        x_again = [sem(f"x_again{k}") for k in range(2)]
        attended = sem("attended")
        result = sem("result")
        stored = sem("stored")

        def k_slot(head, b):
            return NB + b if head % 2 and b < 2 else b

        def columns(t):
            return P * (t.kt % TB) if t.kt // TB == t.g else 0

        def tiles_until(gi):
            return sum(TB * (k % NB + 1) for k in range(gi + 1))

        def mm3(dst, w_hi, w_lo, m_hi, m_lo, first=True, last=True):
            nc.tensor.matmul(dst, w_hi, m_hi, start=first, stop=False)
            nc.tensor.matmul(dst, w_hi, m_lo, start=False, stop=False)
            return nc.tensor.matmul(dst, w_lo, m_hi, start=False, stop=last)

        def ffn_banks(b):
            return ps[:, TB * (b % 2):TB * (b % 2 + 1), :]

        def routed_T(b):
            return ffn_banks(b + 1)[:, TB - 1, :].rearrange("p (t n) -> p t n", t=TB)

        def f32(ap):
            return ap.bitcast(F32)

        def evacuated(job):
            src = aux[job.aux % AUX_BANKS]
            if isinstance(job, Normed):
                cols = slice(job.b * BW, (job.b + 1) * BW)
                return src, xT_hi[:, job.c, cols], xT_lo[:, job.c, cols]
            if isinstance(job, ProjectV):
                t = TB * job.b + 2 * job.half
                return (src.rearrange("p (t n) -> p t n", t=2), v_hi[:, t:t + 2, :], v_lo[:, t:t + 2, :])
            hi, lo = (qT_hi, qT_lo) if job.which == "q" else (kT_hi, kT_lo)
            slot = job.b if job.which == "q" else k_slot(job.head, job.b)
            return src, hi[:, slot, :], lo[:, slot, :]

        block = ctx.enter_context(nc.Block())

        @block.sync
        def _(sp):
            xt = x[0].rearrange("(b t p) d -> b p t d", p=P, t=TB)
            for b in range(NB):
                sp.dma_start(acc[:, TB * b:TB * (b + 1), :], xt[b]).then_inc(x_in[b], 16)
                if b == 0:
                    sp.dma_start(wraw[:, 0, :], wqk[:, 0, :]).then_inc(wqk_in, 16)
                    sp.dma_start(wraw[:, 1, :], wv[:, 0, :]).then_inc(wv_in, 16)
                    sp.dma_start(wraw[:, 2, :], wo[:, 0, :]).then_inc(wo_in, 16)

            def loads(i, last):
                sp.wait_ge(wqk_ready, 2 * i + 1)
                sp.dma_start(wraw[:, 0, :], wqk[:, 2 * i + 1, :] if last else
                             wqk[:, bass.ds(2 * i + 1, 1), :].rearrange("p a n -> p (a n)")).then_inc(wqk_in, 16)
                if last:
                    return
                for raw, src, ready, arrived in ((1, wv, wv_ready, wv_in), (2, wo, wo_ready, wo_in)):
                    sp.wait_ge(ready, i + 1)
                    sp.dma_start(wraw[:, raw, :], src[:, bass.ds(i + 1, 1), :].rearrange("p a n -> p (a n)"))\
                      .then_inc(arrived, 16)
                sp.wait_ge(wqk_ready, 2 * i + 2)
                sp.dma_start(wraw[:, 0, :], wqk[:, bass.ds(2 * i + 2, 1), :].rearrange("p a n -> p (a n)"))\
                  .then_inc(wqk_in, 16)

            with sp.Fori(0, PAIRS - 1) as i:
                loads(i, False)
            loads(PAIRS - 1, True)
            sp.wait_ge(wqk_ready, H)
            sp.wait_ge(wv_ready, PAIRS)
            sp.wait_ge(wo_ready, PAIRS)
            for c in range(DC):
                sp.dma_start(wraw[:, c, 0:FW], ffn_w[:, c, :]).then_inc(ffn_in, 16)
            sp.dma_start(wraw[:, 2, 0:D], lora_b).then_inc(ffn_in, 16)
            sp.dma_start(wraw[:, 2, D:2 * D], bias.partition_broadcast(P)).then_inc(ffn_in, 16)
            out_t = out[0].rearrange("(b t p) d -> b p t d", p=P, t=TB)
            sp.wait_ge(lo_ready, PAIRS * TILES)
            sp.wait_ge(sum_done, PAIRS * TILES)
            for b in range(NB):
                k = b % 2
                if b >= 2:
                    sp.wait_ge(result, b - 1)
                sp.dma_start(probs[:, 2 * k:2 * k + 2, :].rearrange("p a (t d) -> p (a t) d", d=D), xt[b])\
                  .then_inc(x_again[k], 16)
                if b:
                    sp.wait_ge(result, b)
                    sp.dma_start(out_t[b - 1], acc[:, TB * (b - 1):TB * b, :]).then_inc(stored, 16)
            sp.wait_ge(result, NB)
            sp.dma_start(out_t[NB - 1], acc[:, TB * (NB - 1):, :]).then_inc(stored, 16)
            sp.wait_ge(stored, 16 * NB)

        @block.gpsimd
        def _(pool):
            splits = [0]

            def split_weights(raw, hi, lo, arrived, count, nth, ready):
                pool.wait_ge(arrived, count)
                nc.gpsimd.tensor_tensor(hi, raw, zeros[:, 0:1].broadcast_to([P, raw.shape[-1]]), ALU.add)\
                  .then_inc(weight_hi, 1)
                pool.wait_ge(weight_hi, nth)
                nc.gpsimd.tensor_tensor(lo, raw, f32(hi), ALU.subtract).then_inc(ready, 1)

            def flat(t):
                return t.rearrange("p a b -> p (a b)") if len(t.shape) == 3 else t.rearrange("p a b c -> p (a b c)")

            nc.gpsimd.memset(ident[:, :], 0.0).then_inc(made, 1)
            nc.gpsimd.memset(neg_ident[:, :], 0.0).then_inc(made, 1)
            nc.gpsimd.memset(ident_bf[:, :], 0.0).then_inc(made, 1)
            nc.gpsimd.memset(mask_bf[:, :], 0.0).then_inc(made, 1)
            nc.gpsimd.memset(mask_rows[:, :], 0.0).then_inc(made, 1)
            nc.gpsimd.memset(zeros[:, :], 0.0)
            nc.gpsimd.memset(ones[:, :], 1.0).then_inc(made, 1)
            for e in range(E):
                nc.gpsimd.memset(rank[:, :, e:e + 1], float(E - e))
            pool.wait_ge(made, 6)
            diagonal = dict(compare_op=ALU.not_equal, base=0, pattern=[[-1, P]], channel_multiplier=1)
            nc.gpsimd.affine_select(out=ident[:, :], in_=ident[:, :], fill=1.0, **diagonal)
            nc.gpsimd.affine_select(out=neg_ident[:, :], in_=neg_ident[:, :], fill=-1.0, **diagonal)
            nc.gpsimd.affine_select(out=ident_bf[:, :], in_=ident_bf[:, :], fill=1.0, **diagonal)
            nc.gpsimd.affine_select(out=mask_bf[:, :], in_=mask_bf[:, :], compare_op=ALU.is_ge, fill=MASKED,
                                    base=0, pattern=[[1, P]], channel_multiplier=-1)
            nc.gpsimd.affine_select(out=mask_rows[:, BW - P:], in_=mask_rows[:, BW - P:], compare_op=ALU.is_ge,
                                    fill=MASKED, base=0, pattern=[[-1, P]], channel_multiplier=1)
            nc.gpsimd.tensor_copy(ones_r[:, :], ones[:, :]).then_inc(consts, 1)
            split_weights(wraw[:, 0, :], flat(wqk_hi[:, 0]), flat(wqk_lo[:, 0]), wqk_in, 16, 1, wqk_ready)
            split_weights(wraw[:, 1, :], flat(wv_hi[:, :, :]), flat(wv_lo[:, :, :]), wv_in, 16, 2, wv_ready)

            def make_shift(job, block_no):
                pool.wait_ge(max_ready, block_no)
                k = job.g
                nc.gpsimd.tensor_tensor(
                    shift[:, k, :, :], neg_ident[:, None, :].broadcast_to([P, TB, P]),
                    rowmax[:, k, :][:, :, None].broadcast_to([P, TB, P]), ALU.mult).then_inc(shift_ready, 1)

            AHEAD = len([job for job in start_plan if isinstance(job, RowMax) and job.last])
            pool.wait_ge(aux_full, len([job for job in start_plan if isinstance(job, Normed)]))
            nc.gpsimd.memset(acc[:, :, :], 0.0).then_inc(acc_zero, 1)
            for job in start_plan:
                if isinstance(job, RowMax) and job.last:
                    make_shift(job, job.g + 1)

            def pair(i, plan, last):
                groups = AHEAD
                for job in plan:
                    if isinstance(job, RowMax) and job.last:
                        groups += 1
                        make_shift(job, i * GROUPS + groups)
                    if not isinstance(job, Score):
                        continue
                    n, c0 = job.n, columns(job)
                    gi = job.head * NB + job.g
                    total, tile = colsum[:, gi % 2, :], probs[:, n % PROBS, :]
                    pool.wait_ge(probs_ready, i * TILES + n + 1)
                    if job.kt == 0:
                        if job.g == 0:
                            nc.gpsimd.tensor_tensor(total[:, 0:P], tile[:, 0:P], zeros[:, :], ALU.add)
                    elif job.kt == 1:
                        before = probs[:, (n - 1) % PROBS, :]
                        nc.gpsimd.tensor_tensor(total[:, c0:], before[:, c0:], tile[:, c0:], ALU.add)\
                          .then_inc(sum_done, 2)
                    else:
                        pool.wait_ge(sum_done, i * TILES + n)
                        nc.gpsimd.tensor_tensor(total[:, c0:], total[:, c0:], tile[:, c0:], ALU.add)\
                          .then_inc(sum_done, 1)
                    hi_no = 4 * i + 2
                    if n == 1:
                        split_weights(wraw[:, 2, :], flat(wo_hi[:, :, :]), flat(wo_lo[:, :, :]),
                                      wo_in, 16 * (i + 1), hi_no + 1, wo_ready)
                    if n == 6:
                        split_weights(wraw[:, 0, :], flat(wqk_hi[:, 1]), flat(wqk_lo[:, 1]),
                                      wqk_in, 16 * (2 * i + 2), hi_no + 2, wqk_ready)
                    if last:
                        for k, (at, raw, w_hi, w_lo) in enumerate((
                                (6, wraw[:, 0, 0:FW], flat(wqk_hi[:, 0])[:, 0:FW], flat(wqk_lo[:, 0])[:, 0:FW]),
                                (10, wraw[:, 2, 0:D], wv_hi[:, 0, :], wv_lo[:, 0, :]),
                                (14, wraw[:, 2, D:2 * D], wv_hi[:, 1, :], wv_lo[:, 1, :]),
                                (18, wraw[:, 1, 0:FW], flat(wqk_hi[:, 1])[:, 0:FW], flat(wqk_lo[:, 1])[:, 0:FW]))):
                            if n == TILES // 2 + at:
                                split_weights(raw, w_hi, w_lo, ffn_in, 64, hi_no + 3 + k, ffn_w_ready)
                    if n == TILES // 2 + 6 and not last:
                        split_weights(wraw[:, 0, :], flat(wqk_hi[:, 0]), flat(wqk_lo[:, 0]),
                                      wqk_in, 16 * (2 * i + 3), hi_no + 3, wqk_ready)
                    if n == TILES // 2 + 14 and not last:
                        split_weights(wraw[:, 1, :], flat(wv_hi[:, :, :]), flat(wv_lo[:, :, :]),
                                      wv_in, 16 * (i + 2), hi_no + 4, wv_ready)

            with pool.Fori(0, PAIRS - 1) as i:
                pair(i, pair_plan, False)
            pair(PAIRS - 1, last_plan, True)

        @block.scalar
        def _(act):
            act.wait_ge(moments_done, 1)
            nc.scalar.activation(rstd[:, 1, :], rstd[:, 0, :], ACT.Sqrt).then_inc(sqrt_done, 1)

            def walk(plan, i, aux0, ev0):
                groups = 0
                for job in plan:
                    if isinstance(job, (Normed, Project, ProjectV)):
                        src, hi, _ = evacuated(job)
                        act.wait_ge(aux_full, aux0 + job.aux + 1)
                        nc.scalar.activation(hi, src, ACT.Copy).then_inc(aux_hi, 1)
                    elif isinstance(job, Score):
                        n, c0 = job.n, columns(job)
                        k = n % PROBS
                        act.wait_ge(scores_ready, i * TILES + n + 1)
                        if n >= PROBS:
                            act.wait_ge(sum_done, i * TILES + n - PROBS + 1)
                        src = st[n % SCORE_BANKS][:, c0:]
                        nc.scalar.activation(probs[:, k, c0:], src, ACT.Exp, scale=SCALE).then_inc(probs_ready, 1)
                        nc.scalar.activation(p_hi[:, k, c0:], src, ACT.Exp, scale=SCALE).then_inc(hi_ready, 1)
                    elif isinstance(job, SplitZ):
                        groups += 1
                        act.wait_ge(z_full, i * GROUPS + groups)
                        nc.scalar.activation(z_hi[:, :], zb[job.gi % 2], ACT.Copy).then_inc(z_hi_ready, 1)
                        act.wait_ge(sum_done, i * TILES + tiles_until(job.gi))
                        nc.scalar.activation(cs_hi[:, :], colsum[:, job.gi % 2, :], ACT.Copy)\
                          .then_inc(cs_hi_ready, 1)

            walk(start_plan, 0, 0, 0)
            with act.Fori(0, PAIRS - 1) as i:
                walk(pair_plan, i, START_AUX + i * PAIR_AUX, 0)
            walk(last_plan, PAIRS - 1, START_AUX + (PAIRS - 1) * PAIR_AUX, 0)

            for b in range(NB):
                act.wait_ge(routedT, b + 1)
                nc.scalar.activation(rT_hi[:, :, :], routed_T(b), ACT.Copy).then_inc(routedT_hi, 1)
                act.wait_ge(lora_done, b + 1)
                if b >= 2:
                    act.wait_ge(attended, b - 1)
                nc.scalar.activation(gate[:, b % 2, :, :], ffn_banks(b)[:, :, 0:D], ACT.Silu).then_inc(gated, 1)

        @block.vector
        def _(dve):
            for b in range(NB):
                dve.wait_ge(x_in[b], 16)
                for t in range(TB * b, TB * (b + 1)):
                    op = nc.vector.bn_stats(stats[:, t, :], acc[:, t, :])
            op.then_inc(normed, 1)
            dve.wait_ge(normed, 1)
            for t in range(NT):
                op = nc.vector.bn_aggr(moments[:, t, :], stats[:, t, :])
            op.then_inc(normed, 1)
            dve.wait_ge(normed, 2)
            nc.vector.tensor_scalar(rstd[:, 0, :], moments[:, :, 1], EPS, None, ALU.add).then_inc(moments_done, 1)
            dve.wait_ge(sqrt_done, 1)
            r, v = rstd[:, 2, :], rstd[:, 0, :]
            nc.vector.reciprocal(r, rstd[:, 1, :]).then_inc(normed, 1)
            dve.wait_ge(normed, 3)
            nc.vector.tensor_tensor(rstd[:, 3, :], r, r, ALU.mult).then_inc(normed, 1)
            dve.wait_ge(normed, 4)
            nc.vector.scalar_tensor_tensor(rstd[:, 4, :], rstd[:, 3, :], -0.5, v, ALU.mult, ALU.mult)\
              .then_inc(normed, 1)
            dve.wait_ge(normed, 5)
            nc.vector.scalar_tensor_tensor(rstd[:, 5, :], rstd[:, 4, :], 1.5, r, ALU.add, ALU.mult)\
              .then_inc(normed, 1)
            dve.wait_ge(normed, 6)
            for t in range(NT):
                nc.vector.tensor_scalar(acc[:, t, :], acc[:, t, :], moments[:, t, 0:1], rstd[:, 5, t:t + 1],
                                        ALU.subtract, ALU.mult).then_inc(normed, 1)
            dve.wait_ge(consts, 1)

            def lo_part(i, n, c0):
                k = n % PROBS
                dve.wait_ge(hi_ready, i * TILES + n + 1)
                nc.vector.tensor_tensor(p_lo[:, k, c0:], probs[:, k, c0:], f32(p_hi[:, k, c0:]), ALU.subtract)\
                  .then_inc(lo_ready, 1)

            def walk(plan, i, aux0, ev0, maxima, first_groups):
                waiting, groups = [], 0
                for job in plan:
                    if isinstance(job, (Normed, Project, ProjectV)):
                        src, hi, lo = evacuated(job)
                        dve.wait_ge(aux_hi, ev0 + job.ev + 1)
                        nc.vector.tensor_tensor(lo, src, f32(hi), ALU.subtract).then_inc(aux_free, 1)
                    elif isinstance(job, RowMax):
                        src = aux[job.aux % AUX_BANKS]
                        dst = partmax[:, job.g, job.q, job.c:job.c + 1]
                        dve.wait_ge(aux_full, aux0 + job.aux + 1)
                        if job.c < job.g:
                            nc.vector.reduce_max(dst, src, axis=AX).then_inc(aux_free, 1)
                        else:
                            w = P * (job.q + 1)
                            k = job.aux % AUX_BANKS
                            nc.vector.memset(wait_slot[:, k:k + 1], 0.0)
                            nc.vector.tensor_tensor_reduce(
                                out=masked_row[:, k, 0:w], in0=src[:, 0:w], in1=mask_rows[:, BW - w:], scale=1.0,
                                scalar=-3.0e38, op0=ALU.add, op1=ALU.max, accum_out=dst).then_inc(aux_free, 1)
                        if job.last:
                            groups += 1
                            dve.wait_ge(aux_free, aux0 + job.aux + 1)
                            nc.vector.reduce_max(rowmax[:, job.g, :], partmax[:, job.g, :, 0:job.g + 1],
                                                 axis=AX).then_inc(max_ready, 1)
                    elif isinstance(job, Score):
                        if waiting:
                            lo_part(i, *waiting.pop(0))
                        waiting.append((job.n, columns(job)))
                    elif isinstance(job, Value):
                        while waiting and waiting[0][0] <= job.n:
                            lo_part(i, *waiting.pop(0))
                    elif isinstance(job, SplitZ):
                        done = i * GROUPS + job.gi + 1
                        dve.wait_ge(z_hi_ready, done)
                        nc.vector.tensor_tensor(z_lo[:, :], zb[job.gi % 2], f32(z_hi[:, :]), ALU.subtract)\
                          .then_inc(z_lo_ready, 1)
                        dve.wait_ge(cs_hi_ready, done)
                        nc.vector.tensor_tensor(cs_lo[:, :], colsum[:, job.gi % 2, :], f32(cs_hi[:, :]),
                                                ALU.subtract).then_inc(cs_lo_ready, 1)
                    elif isinstance(job, Sums):
                        dve.wait_ge(aux_full, aux0 + job.aux + 1)
                        src = aux[job.aux % AUX_BANKS][:, 0:2 * TB].rearrange("p (t k) -> p t k", k=2)
                        nc.vector.reciprocal(rinv[:, job.gi % 2, :], src[:, :, 0]).then_inc(aux_free, 1)
                    elif isinstance(job, Out):
                        dve.wait_ge(aux_full, aux0 + job.aux + 1)
                        if job.half == 0:
                            sums_aux = max(j.aux for j in plan if isinstance(j, Sums) and j.gi == job.gi)
                            dve.wait_ge(aux_free, aux0 + sums_aux + 1)
                        for k in range(2):
                            q = 2 * job.half + k
                            dst = acc[:, TB * (job.gi % NB) + q, :]
                            op = nc.vector.scalar_tensor_tensor(
                                dst, aux[job.aux % AUX_BANKS][:, k * D:(k + 1) * D],
                                rinv[:, job.gi % 2, q:q + 1], dst, ALU.mult, ALU.add)
                        op.then_inc(aux_free, 1)

            walk(start_plan, 0, 0, 0, 0, 0)
            dve.wait_ge(acc_zero, 1)
            with dve.Fori(0, PAIRS - 1) as i:
                walk(pair_plan, i, START_AUX + i * PAIR_AUX, START_EV + i * PAIR_EV, 1, 0)
            walk(last_plan, PAIRS - 1, START_AUX + (PAIRS - 1) * PAIR_AUX, START_EV + (PAIRS - 1) * PAIR_EV, 1, 0)

            def bcast(ap, k):
                return ap[:, :, None].broadcast_to([P, TB, k])

            def route_block(b):
                dve.wait_ge(base_full, b + 1)
                banks, step = ffn_banks(b), 5 * b
                logits = banks[:, :, D:D + E]

                def chain(op):
                    nonlocal step
                    step += 1
                    op.then_inc(routing, 1)
                    dve.wait_ge(routing, step)
                chain(nc.vector.reduce_max(route[:, 0, :, 0], logits, axis=AX))
                chain(nc.vector.tensor_tensor(route[:, 1], logits, bcast(route[:, 0, :, 0], E), ALU.is_equal))
                chain(nc.vector.tensor_tensor(route[:, 2], route[:, 1], rank[:, :, :], ALU.mult))
                chain(nc.vector.reduce_max(route[:, 3, :, 0], route[:, 2], axis=AX))
                chain(nc.vector.tensor_tensor(route[:, 4], route[:, 2], bcast(route[:, 3, :, 0], E), ALU.is_equal))
                for t in range(TB):
                    op = nc.vector.scalar_tensor_tensor(
                        routed[:, t, :].rearrange("p (e r) -> p e r", e=E),
                        banks[:, t, D + E:FW].rearrange("p (e r) -> p e r", e=E), SCALING,
                        route[:, 4, t, :][:, :, None].broadcast_to([P, E, R]), ALU.mult, ALU.mult)
                op.then_inc(routed_ready, 1)

            route_block(0)
            for b in range(NB):
                dve.wait_ge(routedT_hi, b + 1)
                nc.vector.tensor_tensor(rT_lo[:, :, :], routed_T(b), f32(rT_hi[:, :, :]), ALU.subtract)\
                  .then_inc(routedT_lo, 1)
                if b + 1 < NB:
                    route_block(b + 1)
                dve.wait_ge(gated, b + 1)
                k, a = b % 2, acc[:, TB * b:TB * (b + 1), :]
                nc.vector.tensor_tensor(a, a, gate[:, k, :, :], ALU.mult).then_inc(attended, 1)
                dve.wait_ge(attended, b + 1)
                dve.wait_ge(x_again[k], 16 * (b // 2 + 1))
                nc.vector.tensor_tensor(a, a, probs[:, 2 * k:2 * k + 2, :].rearrange("p a (t d) -> p (a t) d", d=D),
                                        ALU.add).then_inc(result, 1)

        @block.tensor
        def _(pe):
            pe.wait_ge(consts, 1)

            def walk(plan, i, aux0, start):
                made = {}
                for job in plan:
                    if hasattr(job, "aux"):
                        dst = aux[job.aux % AUX_BANKS]
                        if not (start and job.aux < AUX_BANKS):
                            pe.wait_ge(aux_free, aux0 + max(job.aux - AUX_BANKS + 1, 0))
                    if isinstance(job, Normed):
                        for t in range(TB):
                            tok = TB * job.b + t
                            pe.wait_ge(normed, 6 + tok + 1)
                            op = nc.tensor.transpose(dst[:, t * P:(t + 1) * P],
                                                     acc[:, tok, job.c * P:(job.c + 1) * P], ident[:, :])
                        op.then_inc(aux_full, 1)
                        made["x", 0, job.b] = job.aux
                    elif isinstance(job, Project):
                        if start:
                            pe.wait_ge(wqk_ready, 1)
                            pe.wait_ge(aux_free, aux0 + made["x", 0, job.b] + 1)
                        else:
                            pe.wait_ge(wqk_ready, 2 * i + job.head + 1)
                        w, par = "qk".index(job.which), job.head % 2
                        cols = slice(job.b * BW, (job.b + 1) * BW)
                        for c in range(DC):
                            op = mm3(dst, wqk_hi[:, par, w, c, :], wqk_lo[:, par, w, c, :],
                                     xT_hi[:, c, cols], xT_lo[:, c, cols], c == 0, c == DC - 1)
                        op.then_inc(aux_full, 1)
                        made[job.which, job.head, job.b] = job.aux
                    elif isinstance(job, ProjectV):
                        pe.wait_ge(wv_ready, i + 1)
                        for t in range(2):
                            tok = TB * job.b + 2 * job.half + t
                            tile = slice(tok * P, (tok + 1) * P)
                            for c in range(DC):
                                op = mm3(dst[:, t * 2 * P:(t + 1) * 2 * P], xT_hi[:, c, tile], xT_lo[:, c, tile],
                                         wv_hi[:, c, :], wv_lo[:, c, :], c == 0, c == DC - 1)
                        op.then_inc(aux_full, 1)
                        made["v", 0, job.b] = job.aux
                    elif isinstance(job, RowMax):
                        if (job.head, job.g, job.c) not in made:
                            made[job.head, job.g, job.c] = job.aux
                            at = max(made.get(("q", job.head, job.g), -1), made.get(("k", job.head, job.c), -1))
                            if at + 1 > 0 or not start:
                                pe.wait_ge(aux_free, aux0 + at + 1)
                        w = P * (job.q + 1) if job.c == job.g else BW
                        nc.tensor.matmul(dst[:, 0:w], qT_hi[:, job.g, job.q * P:(job.q + 1) * P],
                                         kT_hi[:, k_slot(job.head, job.c), 0:w], start=True, stop=True)\
                          .then_inc(aux_full, 1)
                    elif isinstance(job, Score):
                        n, c0 = job.n, columns(job)
                        if job.kt == 0:
                            pe.wait_ge(shift_ready, i * GROUPS + job.head * NB + job.g + 1)
                        if n >= SCORE_BANKS:
                            pe.wait_ge(hi_ready, i * TILES + n - SCORE_BANKS + 1)
                        dst = st[n % SCORE_BANKS][:, c0:]
                        slot, tile = k_slot(job.head, job.kt // TB), slice(P * (job.kt % TB), P * (job.kt % TB + 1))
                        mm3(dst, kT_hi[:, slot, tile], kT_lo[:, slot, tile], qT_hi[:, job.g, c0:],
                            qT_lo[:, job.g, c0:], True, False)
                        if job.kt // TB == job.g:
                            nc.tensor.matmul(dst[:, 0:P], ident_bf[:, :], mask_bf[:, :], start=False, stop=False)
                        nc.tensor.matmul(dst, ones_r[:, :],
                                         shift[:, job.g, :, :].rearrange("p t n -> p (t n)")[:, c0:],
                                         start=False, stop=True).then_inc(scores_ready, 1)
                    elif isinstance(job, Value):
                        n, c0 = job.n, columns(job)
                        gi, k = job.head * NB + job.g, n % PROBS
                        at = made.get(("v", 0, job.kt // TB))
                        if job.head == 0 and job.kt == TB * job.g:
                            pe.wait_ge(aux_free, aux0 + at + 1)
                        pe.wait_ge(lo_ready, i * TILES + n + 1)
                        dst = zb[gi % 2][:, c0:]
                        cols = slice(P * job.head, P * (job.head + 1))
                        op = mm3(dst, v_hi[:, job.kt, cols], v_lo[:, job.kt, cols], p_hi[:, k, c0:],
                                 p_lo[:, k, c0:], job.kt == 0, job.kt == TB * (job.g + 1) - 1)
                        if job.kt == TB * (job.g + 1) - 1:
                            op.then_inc(z_full, 1)
                    elif isinstance(job, Base):
                        pe.wait_ge(ffn_w_ready, DC + 2)
                        pe.wait_ge(hi_ready, PAIRS * TILES)
                        base(job.b, range(TB))
                    elif isinstance(job, Sums):
                        pe.wait_ge(cs_lo_ready, i * GROUPS + job.gi + 1)
                        for q in range(TB):
                            tile = slice(q * P, (q + 1) * P)
                            nc.tensor.matmul(dst[:, 2 * q:2 * q + 2], cs_hi[:, tile], ones_r[:, 0:2],
                                             start=True, stop=False)
                            op = nc.tensor.matmul(dst[:, 2 * q:2 * q + 2], cs_lo[:, tile], ones_r[:, 0:2],
                                                  start=False, stop=True)
                        op.then_inc(aux_full, 1)
                    elif isinstance(job, Out):
                        pe.wait_ge(wo_ready, i + 1)
                        pe.wait_ge(z_lo_ready, i * GROUPS + job.gi + 1)
                        for k in range(2):
                            tile = slice((2 * job.half + k) * P, (2 * job.half + k + 1) * P)
                            op = mm3(dst[:, k * D:(k + 1) * D], z_hi[:, tile], z_lo[:, tile],
                                     wo_hi[:, job.gi // NB, :], wo_lo[:, job.gi // NB, :])
                        op.then_inc(aux_full, 1)

            def base(b, tiles):
                for t in tiles:
                    tok = TB * b + t
                    tile = slice(tok * P, (tok + 1) * P)
                    for c in range(DC):
                        w_hi, w_lo = (w[:, c].rearrange("p a b c -> p (a b c)")[:, 0:FW] for w in (wqk_hi, wqk_lo))
                        op = mm3(ffn_banks(b)[:, t, 0:FW], xT_hi[:, c, tile], xT_lo[:, c, tile], w_hi, w_lo,
                                 c == 0, c == DC - 1)
                    for w in (wv_hi, wv_lo):
                        op = nc.tensor.matmul(ffn_banks(b)[:, t, 0:D], ones_r[0:1, :], w[0:1, 1, :],
                                              start=False, stop=True, skip_group_check=True)
                if t == TB - 1:
                    op.then_inc(base_full, 1)

            walk(start_plan, 0, 0, True)
            with pe.Fori(0, PAIRS - 1) as i:
                walk(pair_plan, i, START_AUX + i * PAIR_AUX, False)
            walk(last_plan, PAIRS - 1, START_AUX + (PAIRS - 1) * PAIR_AUX, False)

            pe.wait_ge(aux_free, START_AUX + (PAIRS - 1) * PAIR_AUX + LAST_AUX)
            for b in range(NB):
                if b:
                    pe.wait_ge(gated, b)
                if b + 1 < NB:
                    base(b + 1, (0, 1))
                pe.wait_ge(routed_ready, b + 1)
                for t in range(TB):
                    op = nc.tensor.transpose(routed_T(b)[:, t, :], routed[:, t, :], ident[:, :])
                op.then_inc(routedT, 1)
                if b + 1 < NB:
                    base(b + 1, (2,))
                pe.wait_ge(routedT_lo, b + 1)
                for t in range(TB):
                    dst = ffn_banks(b)[:, t, 0:D]
                    for k, (a, w) in enumerate(((rT_hi, wv_hi), (rT_hi, wv_lo), (rT_lo, wv_hi))):
                        op = nc.tensor.matmul(dst, a[:, t, :], w[:, 0, :], start=False, stop=k == 2,
                                              skip_group_check=True)
                op.then_inc(lora_done, 1)
                if b + 1 < NB:
                    base(b + 1, (3,))


def kernel(L0_attn_x, L0_attn_W_K, L0_attn_W_Q, L0_attn_W_V, L0_attn_W_O, L0_ffn_W_base, L0_ffn_b_base,
           L0_ffn_router_W, L0_ffn_A, L0_ffn_Bw):
    import numpy as np
    import concourse.bacc as bacc
    from concourse.bass_utils import run_bass_kernel_spmd

    f = np.ascontiguousarray
    x = f(np.asarray(L0_attn_x))
    H, Dh, D = L0_attn_W_Q.shape
    DC = D // 128

    def chunked(w):
        w = np.asarray(w)
        w = w.reshape(w.shape[:-1] + (DC, 128))
        return np.moveaxis(w, (-1, -2), (0, -2))

    wqk = f(np.stack([chunked(L0_attn_W_Q), chunked(L0_attn_W_K)], axis=2)).reshape(128, H, 2 * DC * Dh)
    wv = chunked(np.asarray(L0_attn_W_V).reshape(H // 2, 2 * Dh, D))
    wv = f(wv).reshape(128, H // 2, DC * 2 * Dh)
    wo = f(np.asarray(L0_attn_W_O).reshape(D, H, Dh).transpose(2, 1, 0)).reshape(Dh, H // 2, 2 * D)
    E, R, _ = L0_ffn_A.shape
    ffn_w = np.concatenate([np.asarray(L0_ffn_W_base), np.asarray(L0_ffn_router_W),
                            np.asarray(L0_ffn_A).reshape(E * R, D)], axis=0)
    ffn_w = f(chunked(ffn_w))
    lora_b = f(np.asarray(L0_ffn_Bw).transpose(0, 2, 1)).reshape(E * R, D)
    arrays = {"x": x, "wqk": wqk, "wv": wv, "wo": wo, "ffn_w": ffn_w, "lora_b": lora_b,
              "bias": f(np.asarray(L0_ffn_b_base))}

    nc = bacc.Bacc("TRN2", target_bir_lowering=False, num_devices=1)
    args = [nc.dram_tensor(f"{n}_dram", a.shape, mybir.dt.from_np(a.dtype), kind="ExternalInput").ap()
            for n, a in arrays.items()]
    out = nc.dram_tensor("out_dram", x.shape, mybir.dt.from_np(x.dtype), kind="ExternalOutput").ap()
    attention_layer(nc, *args, out)
    r = run_bass_kernel_spmd(nc, [{f"{n}_dram": a for n, a in arrays.items()}], core_ids=[0])
    return r.results[0]["out_dram"]
```

```python
from collections import namedtuple
from contextlib import ExitStack

import concourse.bass as bass
from concourse import mybir

ALU = mybir.AluOpType
ACT = mybir.ActivationFunctionType
AX = mybir.AxisListType.X
F32 = mybir.dt.float32
F32R = mybir.dt.float32r
BF16 = mybir.dt.bfloat16

P = 128
TB = 4
BW = TB * P
LAG = 3
PROBS = LAG + 1
SCORE_BANKS = 3
AUX_BANKS = 3
MASKED = -1.0e10
SCALING = 2.0
EPS = 1e-5

Score = namedtuple("Score", "n head g kt")
Value = namedtuple("Value", "n head g kt")
RowMax = namedtuple("RowMax", "aux head g q c last")
Project = namedtuple("Project", "aux ev which head b")
ProjectV = namedtuple("ProjectV", "aux ev b half")
SplitZ = namedtuple("SplitZ", "gi")
Sums = namedtuple("Sums", "aux gi")
Out = namedtuple("Out", "aux gi half")
Normed = namedtuple("Normed", "aux ev c b")
Spread = namedtuple("Spread", "aux head g")
Base = namedtuple("Base", "b")


def number(kinds):
    plan, aux, ev = [], 0, 0
    for kind, args in kinds:
        if kind in (Normed, Project, ProjectV):
            plan.append(kind(aux, ev, *args))
            ev += 1
        elif kind in (RowMax, Spread, Sums, Out):
            plan.append(kind(aux, *args))
        else:
            plan.append(kind(*args))
            continue
        aux += 1
    return plan, aux, ev


def row_maxes(head, g, blocks=None):
    return [(RowMax, (head, g, q, c)) for c in (range(g + 1) if blocks is None else blocks) for q in range(TB)]


def mark_last(kinds):
    left = {}
    for kind, args in kinds:
        if kind is RowMax:
            left[args[:2]] = left.get(args[:2], 0) + 1
    whole = {args[:2] for kind, args in kinds if kind is RowMax and args[3] == args[1]}
    marked = []
    for kind, args in kinds:
        if kind is RowMax:
            left[args[:2]] -= 1
            args += (left[args[:2]] == 0 and args[:2] in whole,)
        marked.append((kind, args))
    return marked


def plan_start(NB):
    kinds = [(Normed, (c, b)) for b in range(NB) for c in range(2)]
    kinds += [(Project, (w, 0, b)) for b in range(2) for w in "kq"] + [(Project, ("q", 0, 2))]
    return number(mark_last(kinds + row_maxes(0, 0) + row_maxes(0, 1) + row_maxes(0, 2, (0, 1))))


SCHEDULE = (
    "V00 | V01 | V10 | v | "
    "Pk03 Pk02 v Pq03 | v | M0222 v M0232 Z0 V11 | M0212 V21 v | M0300 v M0311 S0 M0202 | M0332 v | M0322 v "
    "M0310 O00 O01 | M0301 v B02 | "
    "M0312 v M0331 | v M0303 | M0320 v M0321 Z1 | v Pk10 M0333 | S1 v | M0302 v Pq10 Pq11 | V20 v | v M0330 "
    "M0323 | v M1030 M0313 | V30 v | v M1020 | M1100 B03 v O10 | "
    "M1010 v M1130 | v | M1120 O11 v Z2 | Pq12 Pk11 v | v | v M1000 V31 | v M1101 M1110 | v M1111 S2 | M1221 "
    "v | v M1200 | M1230 v | M1220 v | v M1121 | M1211 v M1131 | v M1210 | v M1231 M1201 | "
    "v | O20 v | O21 v Z3 | v S3 | "
    "O30 Pk12 v | O31 v | M1212 M1202 v M1222 Z4 | Pq13 M1232 Pk13 v | M1332 M1322 v M1331 | v M1300 B12 "
    "M1321 | v S4 M1302 | v M1320 O40 M1312 | "
    "v M1301 | M1303 v | M1311 O41 v Z5 Pq21 | Pk20 S5 M1323 v | v O50 | v M1310 M1333 Pq20 | v M1313 | v "
    "M1330 | v M2020 | v | M2000 v M2120 M2030 | B13 v M2110 | "
    "M2130 v | M2100 v | M2010 O51 v Z6 | Pk21 v Pq22 | v S6 | M2111 v M2121 | v | M2231 v | M2131 v | v | v "
    "M2101 | v O60 O61 | v | M2211 M2201 v | v | M2200 v v v v M2221 Z7 S7 M2230 M2220 O70 O71 M2210 "
)


def plan_pair(NB, last):
    steps = [(h, g, kt) for h in range(2) for g in range(NB) for kt in range(TB * (g + 1))]
    listed = SCHEDULE.split("|")
    assert len(listed) == len(steps) and len(set(SCHEDULE.split()) - {"|", "v"}) == sum(
        code not in "|v" for code in SCHEDULE.split())
    kinds, values = [], iter(range(len(steps)))
    for n, (step, codes) in enumerate(zip(steps, listed)):
        kinds.append((Score, (n, *step)))
        for code in codes.split():
            what, which = code[0], code[1:]
            if what == "v":
                m = next(values)
                kinds.append((Value, (m, *steps[m])))
            elif what == "P":
                kinds.append((Project, (which[0], int(which[1]), int(which[2]))))
            else:
                kind = {"V": ProjectV, "M": RowMax, "B": Spread, "Z": SplitZ, "S": Sums, "O": Out}[what]
                kinds.append((kind, tuple(int(digit) for digit in which)))
    assert next(values, None) is None
    if last:
        def stays(kind, args):
            return not (kind is Project and args[1] == 2 or kind is RowMax and args[0] == 2)
        kinds = [job for job in kinds if stays(*job)]
        kinds.insert(kinds.index((Sums, (2 * NB - 1,))), (Base, (0,)))
    return number(mark_last(kinds))


def on_vector(score):
    return score.g >= 2 and score.kt < TB * score.g and score.kt % 3 > 0


def attention_layer(nc, x, wqk, wv, wo, ffn_w, lora_b, bias, out):
    S, D = x.shape[1], x.shape[2]
    DC = D // P
    NT, NB = S // P, S // BW
    H = wqk.shape[1]
    PAIRS = H // 2
    E = 8
    R = lora_b.shape[0] // E
    FW = D + E + E * R
    SCALE = float(P) ** -0.5
    assert DC == 2 and NT == TB * NB and H % 2 == 0 and E * R == P

    start_plan, START_AUX, START_EV = plan_start(NB)
    pair_plan, PAIR_AUX, PAIR_EV = plan_pair(NB, False)
    last_plan, LAST_AUX, LAST_EV = plan_pair(NB, True)
    TILES = 2 * TB * NB * (NB + 1) // 2
    GROUPS = 2 * NB

    with ExitStack() as ctx:
        def sb(name, shape, dt=F32):
            return ctx.enter_context(nc.sbuf_tensor(name, shape, dt))

        def sem(name):
            return ctx.enter_context(nc.semaphore(name))

        xT_hi, xT_lo = (sb(f"xT_{s}", [P, DC, S], F32R) for s in ("hi", "lo"))
        kT_hi, kT_lo = (sb(f"kT_{s}", [P, 6, BW], F32R) for s in ("hi", "lo"))
        qT_hi, qT_lo = (sb(f"qT_{s}", [P, NB, BW], F32R) for s in ("hi", "lo"))
        v_hi, v_lo = (sb(f"v_{s}", [P, NT, 2 * P], F32R) for s in ("hi", "lo"))
        probs = sb("probs", [P, PROBS, BW])
        p_hi, p_lo = (sb(f"p_{s}", [P, PROBS, BW], F32R) for s in ("hi", "lo"))
        z_hi, z_lo = (sb(f"z_{s}", [P, BW], F32R) for s in ("hi", "lo"))
        colsum = sb("colsum", [P, 2, BW])
        shift = sb("shift", [P, NB, TB, P], F32R)
        partmax = sb("partmax", [P, NB, TB, NB])
        rowmax = sb("rowmax", [P, NB, TB])
        negmax = sb("negmax", [P, 2, BW])
        rinv = sb("rinv", [P, 2, TB])
        acc = sb("acc", [P, NT, D])
        wraw = sb("wraw", [P, 3, BW])
        wqk_hi, wqk_lo = (sb(f"wqk_{s}", [P, 2, 2, DC, P], F32R) for s in ("hi", "lo"))
        wv_hi, wv_lo = (sb(f"wv_{s}", [P, DC, 2 * P], F32R) for s in ("hi", "lo"))
        wo_hi, wo_lo = (sb(f"wo_{s}", [P, 2, D], F32R) for s in ("hi", "lo"))
        ident = sb("ident", [P, P])
        neg_ident = sb("neg_ident", [P, P])
        ident_bf = sb("ident_bf", [P, P], BF16)
        mask_bf = sb("mask_bf", [P, P], BF16)
        mask_rows = sb("mask_rows", [P, BW])
        zeros = sb("zeros", [P, P])
        wait_slot = sb("wait_slot", [P, AUX_BANKS])
        ones = sb("ones", [P, P])
        ones_r = sb("ones_r", [P, P], F32R)
        stats = sb("stats", [P, NT, 6])
        moments = sb("moments", [P, NT, 2])
        rstd = sb("rstd", [P, 6, NT])
        rank = sb("rank", [P, TB, E])
        route = sb("route", [P, 6, TB, E])
        routed = sb("routed", [P, TB, E * R])
        rT_hi, rT_lo = (sb(f"rT_{s}", [P, TB, P], F32R) for s in ("hi", "lo"))
        gate = sb("gate", [P, 2, TB, D])
        masked_row = gate[:, :, :, :].rearrange("p a t d -> p (a t d)")[:, 0:AUX_BANKS * BW]\
            .rearrange("p (k n) -> p k n", k=AUX_BANKS)

        ps = ctx.enter_context(nc.psum_tensor("ps", [P, 8, BW], F32))
        st = [ps[:, k, :] for k in range(SCORE_BANKS)]
        zb = [ps[:, SCORE_BANKS + k, :] for k in range(2)]
        aux = [ps[:, SCORE_BANKS + 2 + k, :] for k in range(AUX_BANKS)]

        x_in = [sem(f"x_in{b}") for b in range(NB)]
        wqk_in, wv_in, wo_in = sem("wqk_in"), sem("wv_in"), sem("wo_in")
        weight_hi = sem("weight_hi")
        wqk_ready, wv_ready, wo_ready = sem("wqk_ready"), sem("wv_ready"), sem("wo_ready")
        consts = sem("consts")
        made = sem("made")
        moments_done = sem("moments_done")
        sqrt_done = sem("sqrt_done")
        normed = sem("normed")
        acc_zero = sem("acc_zero")
        aux_full = sem("aux_full")
        aux_hi = sem("aux_hi")
        aux_free = sem("aux_free")
        max_ready = sem("max_ready")
        shift_ready = sem("shift_ready")
        scores_ready = sem("scores_ready")
        shifted = sem("shifted")
        probs_ready = sem("probs_ready")
        hi_ready = sem("hi_ready")
        lo_ready = sem("lo_ready")
        sum_done = sem("sum_done")
        z_full = sem("z_full")
        z_hi_ready, z_lo_ready = sem("z_hi_ready"), sem("z_lo_ready")
        rinv_ready = sem("rinv_ready")
        ffn_in = sem("ffn_in")
        ffn_w_ready = sem("ffn_w_ready")
        base_full = sem("base_full")
        routing = sem("routing")
        routed_ready = sem("routed_ready")
        routedT = sem("routedT")
        routedT_hi, routedT_lo = sem("routedT_hi"), sem("routedT_lo")
        lora_done = sem("lora_done")
        gated = sem("gated")
        x_again = [sem(f"x_again{k}") for k in range(2)]
        attended = sem("attended")
        result = sem("result")
        stored = sem("stored")

        def k_slot(head, b):
            return NB + b if head % 2 and b < 2 else b

        def shifts_before(n):
            return sum(on_vector(job) for job in pair_plan if isinstance(job, Score) and job.n < n)

        def columns(t):
            return P * (t.kt % TB) if t.kt // TB == t.g else 0

        def tiles_until(gi):
            return sum(TB * (k % NB + 1) for k in range(gi + 1))

        def mm3(dst, w_hi, w_lo, m_hi, m_lo, first=True, last=True):
            nc.tensor.matmul(dst, w_hi, m_hi, start=first, stop=False)
            nc.tensor.matmul(dst, w_hi, m_lo, start=False, stop=False)
            return nc.tensor.matmul(dst, w_lo, m_hi, start=False, stop=last)

        def ffn_banks(b):
            return ps[:, TB * (b % 2):TB * (b % 2 + 1), :]

        def routed_T(b):
            return ffn_banks(b + 1)[:, TB - 1, :].rearrange("p (t n) -> p t n", t=TB)

        def f32(ap):
            return ap.bitcast(F32)

        def evacuated(job):
            src = aux[job.aux % AUX_BANKS]
            if isinstance(job, Normed):
                cols = slice(job.b * BW, (job.b + 1) * BW)
                return src, xT_hi[:, job.c, cols], xT_lo[:, job.c, cols]
            if isinstance(job, ProjectV):
                t = TB * job.b + 2 * job.half
                return (src.rearrange("p (t n) -> p t n", t=2), v_hi[:, t:t + 2, :], v_lo[:, t:t + 2, :])
            hi, lo = (qT_hi, qT_lo) if job.which == "q" else (kT_hi, kT_lo)
            slot = job.b if job.which == "q" else k_slot(job.head, job.b)
            return src, hi[:, slot, :], lo[:, slot, :]

        SHIFTS = shifts_before(TILES)

        block = ctx.enter_context(nc.Block())

        @block.sync
        def _(sp):
            xt = x[0].rearrange("(b t p) d -> b p t d", p=P, t=TB)
            for b in range(NB):
                sp.dma_start(acc[:, TB * b:TB * (b + 1), :], xt[b]).then_inc(x_in[b], 16)
                if b == 0:
                    sp.dma_start(wraw[:, 0, :], wqk[:, 0, :]).then_inc(wqk_in, 16)
                    sp.dma_start(wraw[:, 1, :], wv[:, 0, :]).then_inc(wv_in, 16)
                    sp.dma_start(wraw[:, 2, :], wo[:, 0, :]).then_inc(wo_in, 16)

            def loads(i, last):
                sp.wait_ge(wqk_ready, 2 * i + 1)
                sp.dma_start(wraw[:, 0, :], wqk[:, 2 * i + 1, :] if last else
                             wqk[:, bass.ds(2 * i + 1, 1), :].rearrange("p a n -> p (a n)")).then_inc(wqk_in, 16)
                if last:
                    return
                for raw, src, ready, arrived in ((1, wv, wv_ready, wv_in), (2, wo, wo_ready, wo_in)):
                    sp.wait_ge(ready, i + 1)
                    sp.dma_start(wraw[:, raw, :], src[:, bass.ds(i + 1, 1), :].rearrange("p a n -> p (a n)"))\
                      .then_inc(arrived, 16)
                sp.wait_ge(wqk_ready, 2 * i + 2)
                sp.dma_start(wraw[:, 0, :], wqk[:, bass.ds(2 * i + 2, 1), :].rearrange("p a n -> p (a n)"))\
                  .then_inc(wqk_in, 16)

            with sp.Fori(0, PAIRS - 1) as i:
                loads(i, False)
            loads(PAIRS - 1, True)
            sp.wait_ge(wqk_ready, H)
            sp.wait_ge(wv_ready, PAIRS)
            sp.wait_ge(wo_ready, PAIRS)
            for c in range(DC):
                sp.dma_start(wraw[:, c, 0:FW], ffn_w[:, c, :]).then_inc(ffn_in, 16)
            sp.dma_start(wraw[:, 2, 0:D], lora_b).then_inc(ffn_in, 16)
            sp.dma_start(wraw[:, 2, D:2 * D], bias.partition_broadcast(P)).then_inc(ffn_in, 16)
            out_t = out[0].rearrange("(b t p) d -> b p t d", p=P, t=TB)
            sp.wait_ge(lo_ready, PAIRS * TILES)
            sp.wait_ge(sum_done, PAIRS * TILES)
            for b in range(NB):
                k = b % 2
                if b >= 2:
                    sp.wait_ge(result, b - 1)
                sp.dma_start(probs[:, 2 * k:2 * k + 2, :].rearrange("p a (t d) -> p (a t) d", d=D), xt[b])\
                  .then_inc(x_again[k], 16)
                if b:
                    sp.wait_ge(result, b)
                    sp.dma_start(out_t[b - 1], acc[:, TB * (b - 1):TB * b, :]).then_inc(stored, 16)
            sp.wait_ge(result, NB)
            sp.dma_start(out_t[NB - 1], acc[:, TB * (NB - 1):, :]).then_inc(stored, 16)
            sp.wait_ge(stored, 16 * NB)

        @block.gpsimd
        def _(pool):
            splits = [0]

            def split_weights(raw, hi, lo, arrived, count, nth, ready):
                pool.wait_ge(arrived, count)
                nc.gpsimd.tensor_tensor(hi, raw, zeros[:, 0:1].broadcast_to([P, raw.shape[-1]]), ALU.add)\
                  .then_inc(weight_hi, 1)
                pool.wait_ge(weight_hi, nth)
                nc.gpsimd.tensor_tensor(lo, raw, f32(hi), ALU.subtract).then_inc(ready, 1)

            def flat(t):
                return t.rearrange("p a b -> p (a b)") if len(t.shape) == 3 else t.rearrange("p a b c -> p (a b c)")

            nc.gpsimd.memset(ident[:, :], 0.0).then_inc(made, 1)
            nc.gpsimd.memset(neg_ident[:, :], 0.0).then_inc(made, 1)
            nc.gpsimd.memset(ident_bf[:, :], 0.0).then_inc(made, 1)
            nc.gpsimd.memset(mask_bf[:, :], 0.0).then_inc(made, 1)
            nc.gpsimd.memset(mask_rows[:, :], 0.0).then_inc(made, 1)
            nc.gpsimd.memset(zeros[:, :], 0.0)
            nc.gpsimd.memset(ones[:, :], 1.0).then_inc(made, 1)
            for e in range(E):
                nc.gpsimd.memset(rank[:, :, e:e + 1], float(E - e))
            pool.wait_ge(made, 6)
            diagonal = dict(compare_op=ALU.not_equal, base=0, pattern=[[-1, P]], channel_multiplier=1)
            nc.gpsimd.affine_select(out=ident[:, :], in_=ident[:, :], fill=1.0, **diagonal)
            nc.gpsimd.affine_select(out=neg_ident[:, :], in_=neg_ident[:, :], fill=-1.0, **diagonal)
            nc.gpsimd.affine_select(out=ident_bf[:, :], in_=ident_bf[:, :], fill=1.0, **diagonal)
            nc.gpsimd.affine_select(out=mask_bf[:, :], in_=mask_bf[:, :], compare_op=ALU.is_ge, fill=MASKED,
                                    base=0, pattern=[[1, P]], channel_multiplier=-1)
            nc.gpsimd.affine_select(out=mask_rows[:, BW - P:], in_=mask_rows[:, BW - P:], compare_op=ALU.is_ge,
                                    fill=MASKED, base=0, pattern=[[-1, P]], channel_multiplier=1)
            nc.gpsimd.tensor_copy(ones_r[:, :], ones[:, :]).then_inc(consts, 1)
            split_weights(wraw[:, 0, :], flat(wqk_hi[:, 0]), flat(wqk_lo[:, 0]), wqk_in, 16, 1, wqk_ready)
            split_weights(wraw[:, 1, :], flat(wv_hi[:, :, :]), flat(wv_lo[:, :, :]), wv_in, 16, 2, wv_ready)

            def make_shift(job, block_no):
                pool.wait_ge(max_ready, block_no)
                k = job.g
                nc.gpsimd.tensor_tensor(
                    shift[:, k, :, :], neg_ident[:, None, :].broadcast_to([P, TB, P]),
                    rowmax[:, k, :][:, :, None].broadcast_to([P, TB, P]), ALU.mult).then_inc(shift_ready, 1)

            AHEAD = len([job for job in start_plan if isinstance(job, RowMax) and job.last])
            pool.wait_ge(aux_full, len([job for job in start_plan if isinstance(job, Normed)]))
            nc.gpsimd.memset(acc[:, :, :], 0.0).then_inc(acc_zero, 1)
            for job in start_plan:
                if isinstance(job, RowMax) and job.last:
                    make_shift(job, job.g + 1)

            def pair(i, plan, last):
                groups = AHEAD
                for job in plan:
                    if isinstance(job, RowMax) and job.last:
                        groups += 1
                        make_shift(job, i * GROUPS + groups)
                    if not isinstance(job, Score):
                        continue
                    n, c0 = job.n, columns(job)
                    gi = job.head * NB + job.g
                    total, tile = colsum[:, gi % 2, :], probs[:, n % PROBS, :]
                    pool.wait_ge(probs_ready, i * TILES + n + 1)
                    if job.kt == 0:
                        if job.g == 0:
                            nc.gpsimd.tensor_tensor(total[:, 0:P], tile[:, 0:P], zeros[:, :], ALU.add)
                    elif job.kt == 1:
                        before = probs[:, (n - 1) % PROBS, :]
                        nc.gpsimd.tensor_tensor(total[:, c0:], before[:, c0:], tile[:, c0:], ALU.add)\
                          .then_inc(sum_done, 2)
                    else:
                        pool.wait_ge(sum_done, i * TILES + n)
                        nc.gpsimd.tensor_tensor(total[:, c0:], total[:, c0:], tile[:, c0:], ALU.add)\
                          .then_inc(sum_done, 1)
                    hi_no = 4 * i + 2
                    if n == 1:
                        split_weights(wraw[:, 2, :], flat(wo_hi[:, :, :]), flat(wo_lo[:, :, :]),
                                      wo_in, 16 * (i + 1), hi_no + 1, wo_ready)
                    if n == 6:
                        split_weights(wraw[:, 0, :], flat(wqk_hi[:, 1]), flat(wqk_lo[:, 1]),
                                      wqk_in, 16 * (2 * i + 2), hi_no + 2, wqk_ready)
                    if last:
                        for k, (at, raw, w_hi, w_lo) in enumerate((
                                (6, wraw[:, 0, 0:FW], flat(wqk_hi[:, 0])[:, 0:FW], flat(wqk_lo[:, 0])[:, 0:FW]),
                                (10, wraw[:, 2, 0:D], wv_hi[:, 0, :], wv_lo[:, 0, :]),
                                (14, wraw[:, 2, D:2 * D], wv_hi[:, 1, :], wv_lo[:, 1, :]),
                                (18, wraw[:, 1, 0:FW], flat(wqk_hi[:, 1])[:, 0:FW], flat(wqk_lo[:, 1])[:, 0:FW]))):
                            if n == TILES // 2 + at:
                                split_weights(raw, w_hi, w_lo, ffn_in, 64, hi_no + 3 + k, ffn_w_ready)
                    if n == TILES // 2 + 6 and not last:
                        split_weights(wraw[:, 0, :], flat(wqk_hi[:, 0]), flat(wqk_lo[:, 0]),
                                      wqk_in, 16 * (2 * i + 3), hi_no + 3, wqk_ready)
                    if n == TILES // 2 + 14 and not last:
                        split_weights(wraw[:, 1, :], flat(wv_hi[:, :, :]), flat(wv_lo[:, :, :]),
                                      wv_in, 16 * (i + 2), hi_no + 4, wv_ready)

            with pool.Fori(0, PAIRS - 1) as i:
                pair(i, pair_plan, False)
            pair(PAIRS - 1, last_plan, True)

        @block.scalar
        def _(act):
            act.wait_ge(moments_done, 1)
            nc.scalar.activation(rstd[:, 1, :], rstd[:, 0, :], ACT.Sqrt).then_inc(sqrt_done, 1)

            def walk(plan, i, aux0, ev0):
                groups = 0
                for job in plan:
                    if isinstance(job, (Normed, Project, ProjectV)):
                        src, hi, _ = evacuated(job)
                        act.wait_ge(aux_full, aux0 + job.aux + 1)
                        nc.scalar.activation(hi, src, ACT.Copy).then_inc(aux_hi, 1)
                    elif isinstance(job, Score):
                        n, c0 = job.n, columns(job)
                        k = n % PROBS
                        if on_vector(job):
                            act.wait_ge(shifted, i * SHIFTS + shifts_before(n) + 1)
                        else:
                            act.wait_ge(scores_ready, i * TILES + n + 1)
                        if n >= PROBS:
                            act.wait_ge(sum_done, i * TILES + n - PROBS + 1)
                        src = st[n % SCORE_BANKS][:, c0:]
                        nc.scalar.activation(probs[:, k, c0:], src, ACT.Exp, scale=SCALE).then_inc(probs_ready, 1)
                        nc.scalar.activation(p_hi[:, k, c0:], src, ACT.Exp, scale=SCALE).then_inc(hi_ready, 1)
                    elif isinstance(job, SplitZ):
                        groups += 1
                        act.wait_ge(z_full, i * GROUPS + groups)
                        nc.scalar.activation(z_hi[:, :], zb[job.gi % 2], ACT.Copy).then_inc(z_hi_ready, 1)

            walk(start_plan, 0, 0, 0)
            with act.Fori(0, PAIRS - 1) as i:
                walk(pair_plan, i, START_AUX + i * PAIR_AUX, 0)
            walk(last_plan, PAIRS - 1, START_AUX + (PAIRS - 1) * PAIR_AUX, 0)

            for b in range(NB):
                act.wait_ge(routedT, b + 1)
                nc.scalar.activation(rT_hi[:, :, :], routed_T(b), ACT.Copy).then_inc(routedT_hi, 1)
                act.wait_ge(lora_done, b + 1)
                if b >= 2:
                    act.wait_ge(attended, b - 1)
                nc.scalar.activation(gate[:, b % 2, :, :], ffn_banks(b)[:, :, 0:D], ACT.Silu).then_inc(gated, 1)

        @block.vector
        def _(dve):
            for b in range(NB):
                dve.wait_ge(x_in[b], 16)
                for t in range(TB * b, TB * (b + 1)):
                    op = nc.vector.bn_stats(stats[:, t, :], acc[:, t, :])
            op.then_inc(normed, 1)
            dve.wait_ge(normed, 1)
            for t in range(NT):
                op = nc.vector.bn_aggr(moments[:, t, :], stats[:, t, :])
            op.then_inc(normed, 1)
            dve.wait_ge(normed, 2)
            nc.vector.tensor_scalar(rstd[:, 0, :], moments[:, :, 1], EPS, None, ALU.add).then_inc(moments_done, 1)
            dve.wait_ge(sqrt_done, 1)
            r, v = rstd[:, 2, :], rstd[:, 0, :]
            nc.vector.reciprocal(r, rstd[:, 1, :]).then_inc(normed, 1)
            dve.wait_ge(normed, 3)
            nc.vector.tensor_tensor(rstd[:, 3, :], r, r, ALU.mult).then_inc(normed, 1)
            dve.wait_ge(normed, 4)
            nc.vector.scalar_tensor_tensor(rstd[:, 4, :], rstd[:, 3, :], -0.5, v, ALU.mult, ALU.mult)\
              .then_inc(normed, 1)
            dve.wait_ge(normed, 5)
            nc.vector.scalar_tensor_tensor(rstd[:, 5, :], rstd[:, 4, :], 1.5, r, ALU.add, ALU.mult)\
              .then_inc(normed, 1)
            dve.wait_ge(normed, 6)
            for t in range(NT):
                nc.vector.tensor_scalar(acc[:, t, :], acc[:, t, :], moments[:, t, 0:1], rstd[:, 5, t:t + 1],
                                        ALU.subtract, ALU.mult).then_inc(normed, 1)
            dve.wait_ge(consts, 1)

            def lo_part(i, n, c0):
                k = n % PROBS
                dve.wait_ge(hi_ready, i * TILES + n + 1)
                nc.vector.tensor_tensor(p_lo[:, k, c0:], probs[:, k, c0:], f32(p_hi[:, k, c0:]), ALU.subtract)\
                  .then_inc(lo_ready, 1)

            def walk(plan, i, aux0, ev0, maxima, first_groups):
                waiting, groups, spread_out = [], 0, None
                for job in plan:
                    if isinstance(job, (Normed, Project, ProjectV)):
                        src, hi, lo = evacuated(job)
                        dve.wait_ge(aux_hi, ev0 + job.ev + 1)
                        nc.vector.tensor_tensor(lo, src, f32(hi), ALU.subtract).then_inc(aux_free, 1)
                    elif isinstance(job, RowMax):
                        src = aux[job.aux % AUX_BANKS]
                        dst = partmax[:, job.g, job.q, job.c:job.c + 1]
                        dve.wait_ge(aux_full, aux0 + job.aux + 1)
                        if job.c < job.g:
                            nc.vector.reduce_max(dst, src, axis=AX).then_inc(aux_free, 1)
                        else:
                            w = P * (job.q + 1)
                            k = job.aux % AUX_BANKS
                            nc.vector.memset(wait_slot[:, k:k + 1], 0.0)
                            nc.vector.tensor_tensor_reduce(
                                out=masked_row[:, k, 0:w], in0=src[:, 0:w], in1=mask_rows[:, BW - w:], scale=1.0,
                                scalar=-3.0e38, op0=ALU.add, op1=ALU.max, accum_out=dst).then_inc(aux_free, 1)
                        if job.last:
                            groups += 1
                            dve.wait_ge(aux_free, aux0 + job.aux + 1)
                            nc.vector.reduce_max(rowmax[:, job.g, :], partmax[:, job.g, :, 0:job.g + 1],
                                                 axis=AX).then_inc(max_ready, 1)
                    elif isinstance(job, Spread):
                        dve.wait_ge(aux_full, aux0 + job.aux + 1)
                        nc.vector.tensor_copy(negmax[:, job.g - 2, :], aux[job.aux % AUX_BANKS])\
                          .then_inc(aux_free, 1)
                        spread_out = job.aux
                    elif isinstance(job, Score):
                        if on_vector(job):
                            bank = st[job.n % SCORE_BANKS]
                            if spread_out is not None:
                                dve.wait_ge(aux_free, aux0 + spread_out + 1)
                                spread_out = None
                            dve.wait_ge(scores_ready, i * TILES + job.n + 1)
                            nc.vector.tensor_tensor(bank, bank, negmax[:, job.g - 2, :], ALU.add)\
                              .then_inc(shifted, 1)
                        if waiting:
                            lo_part(i, *waiting.pop(0))
                        waiting.append((job.n, columns(job)))
                    elif isinstance(job, Value):
                        while waiting and waiting[0][0] <= job.n:
                            lo_part(i, *waiting.pop(0))
                    elif isinstance(job, SplitZ):
                        done = i * GROUPS + job.gi + 1
                        dve.wait_ge(z_hi_ready, done)
                        nc.vector.tensor_tensor(z_lo[:, :], zb[job.gi % 2], f32(z_hi[:, :]), ALU.subtract)\
                          .then_inc(z_lo_ready, 1)
                    elif isinstance(job, Sums):
                        dve.wait_ge(aux_full, aux0 + job.aux + 1)
                        nc.vector.reciprocal(rinv[:, job.gi % 2, :], aux[job.aux % AUX_BANKS][:, 0:TB])\
                          .then_inc(aux_free, 1)
                    elif isinstance(job, Out):
                        dve.wait_ge(aux_full, aux0 + job.aux + 1)
                        if job.half == 0:
                            sums_aux = max(j.aux for j in plan if isinstance(j, Sums) and j.gi == job.gi)
                            dve.wait_ge(aux_free, aux0 + sums_aux + 1)
                        for k in range(2):
                            q = 2 * job.half + k
                            dst = acc[:, TB * (job.gi % NB) + q, :]
                            op = nc.vector.scalar_tensor_tensor(
                                dst, aux[job.aux % AUX_BANKS][:, k * D:(k + 1) * D],
                                rinv[:, job.gi % 2, q:q + 1], dst, ALU.mult, ALU.add)
                        op.then_inc(aux_free, 1)

            walk(start_plan, 0, 0, 0, 0, 0)
            dve.wait_ge(acc_zero, 1)
            with dve.Fori(0, PAIRS - 1) as i:
                walk(pair_plan, i, START_AUX + i * PAIR_AUX, START_EV + i * PAIR_EV, 1, 0)
            walk(last_plan, PAIRS - 1, START_AUX + (PAIRS - 1) * PAIR_AUX, START_EV + (PAIRS - 1) * PAIR_EV, 1, 0)

            def bcast(ap, k):
                return ap[:, :, None].broadcast_to([P, TB, k])

            def route_block(b):
                dve.wait_ge(base_full, b + 1)
                banks, step = ffn_banks(b), 5 * b
                logits = banks[:, :, D:D + E]

                def chain(op):
                    nonlocal step
                    step += 1
                    op.then_inc(routing, 1)
                    dve.wait_ge(routing, step)
                chain(nc.vector.reduce_max(route[:, 0, :, 0], logits, axis=AX))
                chain(nc.vector.tensor_tensor(route[:, 1], logits, bcast(route[:, 0, :, 0], E), ALU.is_equal))
                chain(nc.vector.tensor_tensor(route[:, 2], route[:, 1], rank[:, :, :], ALU.mult))
                chain(nc.vector.reduce_max(route[:, 3, :, 0], route[:, 2], axis=AX))
                chain(nc.vector.tensor_tensor(route[:, 4], route[:, 2], bcast(route[:, 3, :, 0], E), ALU.is_equal))
                for t in range(TB):
                    op = nc.vector.scalar_tensor_tensor(
                        routed[:, t, :].rearrange("p (e r) -> p e r", e=E),
                        banks[:, t, D + E:FW].rearrange("p (e r) -> p e r", e=E), SCALING,
                        route[:, 4, t, :][:, :, None].broadcast_to([P, E, R]), ALU.mult, ALU.mult)
                op.then_inc(routed_ready, 1)

            route_block(0)
            for b in range(NB):
                dve.wait_ge(routedT_hi, b + 1)
                nc.vector.tensor_tensor(rT_lo[:, :, :], routed_T(b), f32(rT_hi[:, :, :]), ALU.subtract)\
                  .then_inc(routedT_lo, 1)
                if b + 1 < NB:
                    route_block(b + 1)
                dve.wait_ge(gated, b + 1)
                k, a = b % 2, acc[:, TB * b:TB * (b + 1), :]
                nc.vector.tensor_tensor(a, a, gate[:, k, :, :], ALU.mult).then_inc(attended, 1)
                dve.wait_ge(attended, b + 1)
                dve.wait_ge(x_again[k], 16 * (b // 2 + 1))
                nc.vector.tensor_tensor(a, a, probs[:, 2 * k:2 * k + 2, :].rearrange("p a (t d) -> p (a t) d", d=D),
                                        ALU.add).then_inc(result, 1)

        @block.tensor
        def _(pe):
            pe.wait_ge(consts, 1)

            def walk(plan, i, aux0, start):
                made = {}
                for job in plan:
                    if hasattr(job, "aux"):
                        dst = aux[job.aux % AUX_BANKS]
                        if not (start and job.aux < AUX_BANKS):
                            pe.wait_ge(aux_free, aux0 + max(job.aux - AUX_BANKS + 1, 0))
                    if isinstance(job, Normed):
                        for t in range(TB):
                            tok = TB * job.b + t
                            pe.wait_ge(normed, 6 + tok + 1)
                            op = nc.tensor.transpose(dst[:, t * P:(t + 1) * P],
                                                     acc[:, tok, job.c * P:(job.c + 1) * P], ident[:, :])
                        op.then_inc(aux_full, 1)
                        made["x", 0, job.b] = job.aux
                    elif isinstance(job, Project):
                        if start:
                            pe.wait_ge(wqk_ready, 1)
                            pe.wait_ge(aux_free, aux0 + made["x", 0, job.b] + 1)
                        else:
                            pe.wait_ge(wqk_ready, 2 * i + job.head + 1)
                        w, par = "qk".index(job.which), job.head % 2
                        cols = slice(job.b * BW, (job.b + 1) * BW)
                        for c in range(DC):
                            op = mm3(dst, wqk_hi[:, par, w, c, :], wqk_lo[:, par, w, c, :],
                                     xT_hi[:, c, cols], xT_lo[:, c, cols], c == 0, c == DC - 1)
                        op.then_inc(aux_full, 1)
                        made[job.which, job.head, job.b] = job.aux
                    elif isinstance(job, ProjectV):
                        pe.wait_ge(wv_ready, i + 1)
                        for t in range(2):
                            tok = TB * job.b + 2 * job.half + t
                            tile = slice(tok * P, (tok + 1) * P)
                            for c in range(DC):
                                op = mm3(dst[:, t * 2 * P:(t + 1) * 2 * P], xT_hi[:, c, tile], xT_lo[:, c, tile],
                                         wv_hi[:, c, :], wv_lo[:, c, :], c == 0, c == DC - 1)
                        op.then_inc(aux_full, 1)
                        made["v", 0, job.b] = job.aux
                    elif isinstance(job, RowMax):
                        if (job.head, job.g, job.c) not in made:
                            made[job.head, job.g, job.c] = job.aux
                            at = max(made.get(("q", job.head, job.g), -1), made.get(("k", job.head, job.c), -1))
                            if at + 1 > 0 or not start:
                                pe.wait_ge(aux_free, aux0 + at + 1)
                        w = P * (job.q + 1) if job.c == job.g else BW
                        nc.tensor.matmul(dst[:, 0:w], qT_hi[:, job.g, job.q * P:(job.q + 1) * P],
                                         kT_hi[:, k_slot(job.head, job.c), 0:w], start=True, stop=True)\
                          .then_inc(aux_full, 1)
                    elif isinstance(job, Spread):
                        pe.wait_ge(shift_ready, i * GROUPS + job.head * NB + job.g + 1)
                        nc.tensor.matmul(dst, ones_r[:, :], shift[:, job.g, :, :].rearrange("p t n -> p (t n)"),
                                         start=True, stop=True).then_inc(aux_full, 1)
                    elif isinstance(job, Score):
                        n, c0 = job.n, columns(job)
                        if job.kt == 0:
                            pe.wait_ge(shift_ready, i * GROUPS + job.head * NB + job.g + 1)
                        if n >= SCORE_BANKS:
                            pe.wait_ge(hi_ready, i * TILES + n - SCORE_BANKS + 1)
                        dst = st[n % SCORE_BANKS][:, c0:]
                        slot, tile = k_slot(job.head, job.kt // TB), slice(P * (job.kt % TB), P * (job.kt % TB + 1))
                        op = mm3(dst, kT_hi[:, slot, tile], kT_lo[:, slot, tile], qT_hi[:, job.g, c0:],
                                 qT_lo[:, job.g, c0:], True, on_vector(job))
                        if job.kt // TB == job.g:
                            nc.tensor.matmul(dst[:, 0:P], ident_bf[:, :], mask_bf[:, :], start=False, stop=False)
                        if not on_vector(job):
                            op = nc.tensor.matmul(dst, ones_r[:, :],
                                                  shift[:, job.g, :, :].rearrange("p t n -> p (t n)")[:, c0:],
                                                  start=False, stop=True)
                        op.then_inc(scores_ready, 1)
                    elif isinstance(job, Value):
                        n, c0 = job.n, columns(job)
                        gi, k = job.head * NB + job.g, n % PROBS
                        at = made.get(("v", 0, job.kt // TB))
                        if job.head == 0 and job.kt == TB * job.g:
                            pe.wait_ge(aux_free, aux0 + at + 1)
                        pe.wait_ge(lo_ready, i * TILES + n + 1)
                        dst = zb[gi % 2][:, c0:]
                        cols = slice(P * job.head, P * (job.head + 1))
                        op = mm3(dst, v_hi[:, job.kt, cols], v_lo[:, job.kt, cols], p_hi[:, k, c0:],
                                 p_lo[:, k, c0:], job.kt == 0, job.kt == TB * (job.g + 1) - 1)
                        if job.kt == TB * (job.g + 1) - 1:
                            op.then_inc(z_full, 1)
                    elif isinstance(job, Base):
                        pe.wait_ge(ffn_w_ready, DC + 2)
                        pe.wait_ge(hi_ready, PAIRS * TILES)
                        base(job.b, range(TB))
                    elif isinstance(job, Sums):
                        pe.wait_ge(sum_done, i * TILES + tiles_until(job.gi))
                        for q in range(TB):
                            op = nc.tensor.matmul(dst[:, q:q + 1], colsum[:, job.gi % 2, q * P:(q + 1) * P],
                                                  ones[:, 0:1], start=True, stop=True)
                        op.then_inc(aux_full, 1)
                    elif isinstance(job, Out):
                        pe.wait_ge(wo_ready, i + 1)
                        pe.wait_ge(z_lo_ready, i * GROUPS + job.gi + 1)
                        for k in range(2):
                            tile = slice((2 * job.half + k) * P, (2 * job.half + k + 1) * P)
                            op = mm3(dst[:, k * D:(k + 1) * D], z_hi[:, tile], z_lo[:, tile],
                                     wo_hi[:, job.gi // NB, :], wo_lo[:, job.gi // NB, :])
                        op.then_inc(aux_full, 1)

            def base(b, tiles):
                for t in tiles:
                    tok = TB * b + t
                    tile = slice(tok * P, (tok + 1) * P)
                    for c in range(DC):
                        w_hi, w_lo = (w[:, c].rearrange("p a b c -> p (a b c)")[:, 0:FW] for w in (wqk_hi, wqk_lo))
                        op = mm3(ffn_banks(b)[:, t, 0:FW], xT_hi[:, c, tile], xT_lo[:, c, tile], w_hi, w_lo,
                                 c == 0, c == DC - 1)
                    for w in (wv_hi, wv_lo):
                        op = nc.tensor.matmul(ffn_banks(b)[:, t, 0:D], ones_r[0:1, :], w[0:1, 1, :],
                                              start=False, stop=True, skip_group_check=True)
                if t == TB - 1:
                    op.then_inc(base_full, 1)

            walk(start_plan, 0, 0, True)
            with pe.Fori(0, PAIRS - 1) as i:
                walk(pair_plan, i, START_AUX + i * PAIR_AUX, False)
            walk(last_plan, PAIRS - 1, START_AUX + (PAIRS - 1) * PAIR_AUX, False)

            pe.wait_ge(aux_free, START_AUX + (PAIRS - 1) * PAIR_AUX + LAST_AUX)
            for b in range(NB):
                if b:
                    pe.wait_ge(gated, b)
                if b + 1 < NB:
                    base(b + 1, (0, 1))
                pe.wait_ge(routed_ready, b + 1)
                for t in range(TB):
                    op = nc.tensor.transpose(routed_T(b)[:, t, :], routed[:, t, :], ident[:, :])
                op.then_inc(routedT, 1)
                if b + 1 < NB:
                    base(b + 1, (2,))
                pe.wait_ge(routedT_lo, b + 1)
                for t in range(TB):
                    dst = ffn_banks(b)[:, t, 0:D]
                    for k, (a, w) in enumerate(((rT_hi, wv_hi), (rT_hi, wv_lo), (rT_lo, wv_hi))):
                        op = nc.tensor.matmul(dst, a[:, t, :], w[:, 0, :], start=False, stop=k == 2,
                                              skip_group_check=True)
                op.then_inc(lora_done, 1)
                if b + 1 < NB:
                    base(b + 1, (3,))


def kernel(L0_attn_x, L0_attn_W_K, L0_attn_W_Q, L0_attn_W_V, L0_attn_W_O, L0_ffn_W_base, L0_ffn_b_base,
           L0_ffn_router_W, L0_ffn_A, L0_ffn_Bw):
    import numpy as np
    import concourse.bacc as bacc
    from concourse.bass_utils import run_bass_kernel_spmd

    f = np.ascontiguousarray
    x = f(np.asarray(L0_attn_x))
    H, Dh, D = L0_attn_W_Q.shape
    DC = D // 128

    def chunked(w):
        w = np.asarray(w)
        w = w.reshape(w.shape[:-1] + (DC, 128))
        return np.moveaxis(w, (-1, -2), (0, -2))

    wqk = f(np.stack([chunked(L0_attn_W_Q), chunked(L0_attn_W_K)], axis=2)).reshape(128, H, 2 * DC * Dh)
    wv = chunked(np.asarray(L0_attn_W_V).reshape(H // 2, 2 * Dh, D))
    wv = f(wv).reshape(128, H // 2, DC * 2 * Dh)
    wo = f(np.asarray(L0_attn_W_O).reshape(D, H, Dh).transpose(2, 1, 0)).reshape(Dh, H // 2, 2 * D)
    E, R, _ = L0_ffn_A.shape
    ffn_w = np.concatenate([np.asarray(L0_ffn_W_base), np.asarray(L0_ffn_router_W),
                            np.asarray(L0_ffn_A).reshape(E * R, D)], axis=0)
    ffn_w = f(chunked(ffn_w))
    lora_b = f(np.asarray(L0_ffn_Bw).transpose(0, 2, 1)).reshape(E * R, D)
    arrays = {"x": x, "wqk": wqk, "wv": wv, "wo": wo, "ffn_w": ffn_w, "lora_b": lora_b,
              "bias": f(np.asarray(L0_ffn_b_base))}

    nc = bacc.Bacc("TRN2", target_bir_lowering=False, num_devices=1)
    args = [nc.dram_tensor(f"{n}_dram", a.shape, mybir.dt.from_np(a.dtype), kind="ExternalInput").ap()
            for n, a in arrays.items()]
    out = nc.dram_tensor("out_dram", x.shape, mybir.dt.from_np(x.dtype), kind="ExternalOutput").ap()
    attention_layer(nc, *args, out)
    r = run_bass_kernel_spmd(nc, [{f"{n}_dram": a for n, a in arrays.items()}], core_ids=[0])
    return r.results[0]["out_dram"]
```
